# Optimizing a Trainium2 kernel written in Bass

```python
import numpy as np
import jax
import jax.numpy as jnp

def _softmax(x, axis=-1):
    return jax.nn.softmax(x, axis=axis)

def _gelu(x):
    return jax.nn.gelu(x, approximate=True)

def _silu(x):
    return jax.nn.silu(x)

def _sigmoid(x):
    return jax.nn.sigmoid(x)

def _layernorm(x, axis=-1, eps=1e-05):
    m = jnp.mean(x, axis=axis, keepdims=True)
    v = jnp.var(x, axis=axis, keepdims=True)
    return (x - m) / jnp.sqrt(v + eps)

def _scatter_add(tgt, idx, src, axis=0):
    return tgt.at[idx].add(src)

def _segment_sum(src, seg, n):
    return jax.ops.segment_sum(src, seg, n)
kernel_name = 'mk_adj_preln_d2_adj_r2_9f16a1'

def setup_inputs(seed: int=0):
    np.random.seed(seed)
    _w = jnp.asarray

    def _rec_inputs():
        import jax
        import jax.numpy as jnp
        _gk = jax.random.key(seed)
        x = -0.0002928 + 1 * jax.random.normal(jax.random.fold_in(_gk, 1), (2048, 512), jnp.float32)
        _a = jax.random.bernoulli(jax.random.fold_in(_gk, 2), 0.000976562, (2048, 2048))
        _af = _a.astype(jnp.float32)
        adj = _af
        return (x, adj)
    x, adj = _rec_inputs()

    def _L0_gnn_setup():
        import jax, jax.numpy as jnp
        import numpy as np
        N = 2048
        D_IN = 512
        H = 16
        DH = D_IN // H
        ALPHA = 0.2
        MASK_VAL = -65500.0
        key = jax.random.key(seed)
        ks = jax.random.split(key, 7)
        x = jax.random.normal(ks[0], (N, D_IN), dtype=jnp.float32)
        adj = jax.random.randint(ks[1], (N, N), 0, 2).astype(jnp.float32)
        s = 1.0 / np.sqrt(D_IN)
        W_seq = jax.random.normal(ks[2], (D_IN, D_IN), dtype=jnp.float32) * s
        a1 = jax.random.normal(ks[3], (DH,), dtype=jnp.float32) / np.sqrt(DH)
        a2 = jax.random.normal(ks[4], (DH,), dtype=jnp.float32) / np.sqrt(DH)
        W_out = jax.random.normal(ks[5], (D_IN, D_IN), dtype=jnp.float32) * s
        b_out = jax.random.normal(ks[6], (D_IN,), dtype=jnp.float32) * 0.01
        return {'x': x, 'adj': adj, 'W_seq': W_seq, 'a1': a1, 'a2': a2, 'W_out': W_out, 'b_out': b_out}
    _L0_gnn_all = _L0_gnn_setup()
    _L0_gnn_in = {k: v for k, v in _L0_gnn_all.items() if k in ('W_seq', 'a1', 'a2', 'W_out', 'b_out')}
    del _L0_gnn_all

    def _L1_gnn_setup():
        import jax, jax.numpy as jnp
        import numpy as np
        import math
        SENT_DIM = 512
        N_SENT = 2048
        key = jax.random.key(seed)
        ks = jax.random.split(key, 8)
        D = SENT_DIM
        s = 1.0 / math.sqrt(D)
        return {'sent_embed': jax.random.normal(ks[0], (N_SENT, D), dtype=jnp.float32), 'adj_tensor': jax.random.randint(ks[1], (N_SENT, N_SENT), 0, 2).astype(jnp.float32), 'W_q': jax.random.uniform(ks[2], (D, D), jnp.float32, -s, s), 'b_q': jax.random.uniform(ks[3], (D,), jnp.float32, -s, s), 'W_k': jax.random.uniform(ks[4], (D, D), jnp.float32, -s, s), 'b_k': jax.random.uniform(ks[5], (D,), jnp.float32, -s, s), 'W_v': jax.random.uniform(ks[6], (D, D), jnp.float32, -s, s), 'b_v': jax.random.uniform(ks[7], (D,), jnp.float32, -s, s)}
    _L1_gnn_all = _L1_gnn_setup()
    _L1_gnn_in = {k: v for k, v in _L1_gnn_all.items() if k in ('W_q', 'b_q', 'W_k', 'b_k', 'W_v', 'b_v')}
    del _L1_gnn_all
    return {'x': x, 'adj': adj, 'L0_gnn_W_seq': _L0_gnn_in['W_seq'], 'L0_gnn_a1': _L0_gnn_in['a1'], 'L0_gnn_a2': _L0_gnn_in['a2'], 'L0_gnn_W_out': _L0_gnn_in['W_out'], 'L0_gnn_b_out': _L0_gnn_in['b_out'], 'L1_gnn_W_q': _L1_gnn_in['W_q'], 'L1_gnn_b_q': _L1_gnn_in['b_q'], 'L1_gnn_W_k': _L1_gnn_in['W_k'], 'L1_gnn_b_k': _L1_gnn_in['b_k'], 'L1_gnn_W_v': _L1_gnn_in['W_v'], 'L1_gnn_b_v': _L1_gnn_in['b_v']}

def reference(x, adj, L0_gnn_W_seq, L0_gnn_a1, L0_gnn_a2, L0_gnn_W_out, L0_gnn_b_out, L1_gnn_W_q, L1_gnn_b_q, L1_gnn_W_k, L1_gnn_b_k, L1_gnn_W_v, L1_gnn_b_v):
    import jax
    import jax.numpy as jnp

    def _L0_gnn_ref(x, adj, W_seq, a1, a2, W_out, b_out):
        import jax, jax.numpy as jnp
        import numpy as np
        N = 2048
        D_IN = 512
        H = 16
        DH = D_IN // H
        ALPHA = 0.2
        MASK_VAL = -65500.0
        seq = (x @ W_seq).reshape(N, H, DH)
        score1 = jnp.einsum('nhd,d->hn', seq, a1)
        score2 = jnp.einsum('nhd,d->hn', seq, a2)
        scores = score1[:, :, None] + score2[:, None, :]
        scores = jax.nn.leaky_relu(scores, negative_slope=ALPHA)
        scores = scores + (1.0 - adj)[None, :, :] * MASK_VAL
        attn = jax.nn.softmax(scores, axis=-1)
        hidden = jnp.einsum('hij,jhd->ihd', attn, seq).reshape(N, D_IN)
        hidden = hidden @ W_out + b_out
        return jax.nn.elu(hidden)

    def _L1_gnn_ref(sent_embed, adj_tensor, W_q, b_q, W_k, b_k, W_v, b_v):
        import jax, jax.numpy as jnp
        import numpy as np
        import math
        SENT_DIM = 512
        N_SENT = 2048
        q = sent_embed @ W_q.T + b_q
        k = sent_embed @ W_k.T + b_k
        v = sent_embed @ W_v.T + b_v
        scale = 1.0 / math.sqrt(sent_embed.shape[-1])
        z = scale * (q @ k.T)
        spare_z = z * adj_tensor
        spare_z = jnp.where(spare_z == 0.0, jnp.asarray(-10000.0, spare_z.dtype), spare_z)
        attn = jax.nn.softmax(spare_z, axis=1)
        out = attn @ v
        return jax.nn.relu(out)
    h = jnp.maximum(_layernorm(x, axis=-1), 0.0)
    x = x + _L0_gnn_ref(h, adj, L0_gnn_W_seq, L0_gnn_a1, L0_gnn_a2, L0_gnn_W_out, L0_gnn_b_out)
    h = jnp.maximum(_layernorm(x, axis=-1), 0.0)
    x = x + _L1_gnn_ref(h, adj, L1_gnn_W_q, L1_gnn_b_q, L1_gnn_W_k, L1_gnn_b_k, L1_gnn_W_v, L1_gnn_b_v)
    return x

_drawn_inputs = setup_inputs


def setup_inputs(seed=0):
    import zlib

    import numpy as np

    out = dict(_drawn_inputs(seed))
    spreads = {}
    factors = {'L0_gnn_b_out': 6.891,
     'L1_gnn_W_q': 5.975,
     'L1_gnn_b_q': 38.86,
     'L1_gnn_W_k': 6.163,
     'L1_gnn_b_k': 64.0,
     'L1_gnn_b_v': 3.703}
    for name, (base, spread) in spreads.items():
        noise = np.random.default_rng([zlib.crc32(name.encode()), seed]).standard_normal(out[name].shape)
        drawn = base * np.exp(spread * noise) if base else spread * noise
        out[name] = jnp.asarray(drawn.astype(out[name].dtype))
    for name, factor in factors.items():
        out[name] = (out[name] * factor).astype(out[name].dtype)
    return out
```

```python
from contextlib import ExitStack

import concourse.bass as bass
from concourse import mybir

ALU = mybir.AluOpType
ACT = mybir.ActivationFunctionType
AX_X = mybir.AxisListType.X
F32 = mybir.dt.float32
I32 = mybir.dt.int32
U32 = mybir.dt.uint32

P = 128
N = 2048
D = 512
T = N // P
C = D // P
H = 16
DH = D // H
SX = D + 2 * H
EPS = 1e-5
ALPHA = 0.2
MASK = 65500.0
SCALE = float(D) ** -0.5
RING = 4


def build(nc, x, adj, w_seq_d, a1_d, a2_d, w_out_d, b_out_d, wq_d, bq_d, wk_d, bk_d, wv_d, bv_d, out):
    ctx = ExitStack()
    with ctx:
        def sb(name, shape, dt=F32, stack=ctx):
            return stack.enter_context(nc.sbuf_tensor(name, shape, dt))

        def sem(name):
            return ctx.enter_context(nc.semaphore(name))

        bank = [ctx.enter_context(nc.psum_tensor(f"bank{i}", [P, 512], F32)) for i in range(8)]

        s2t_dram = nc.dram_tensor("s2t_dram", [H, N], F32, kind="Internal").ap()

        ident = sb("ident", [P, P])
        ones = sb("ones", [P, 512])
        w_seq = sb("w_seq", [P, C, D])
        w_out = sb("w_out", [P, C, D])
        w_qk = sb("w_qk", [P, C, D])
        wv_t = sb("wv_t", [P, C, D])
        w_a = sb("w_a", [P, C, 2 * H])
        bout_bc = sb("bout_bc", [P, D])
        bv_bc = sb("bv_bc", [P, D])
        a_bc = sb("a_bc", [P, 2, DH])
        bq_col = sb("bq_col", [P, C])
        bk_col = sb("bk_col", [P, C])
        u_bias = sb("u_bias", [P, C])
        c_vec = sb("c_vec", [P, C])
        bqk = sb("bqk", [1, 1])
        seq_all = sb("seq_all", [P, T, SX])
        stats = sb("stats", [P, RING, 6])
        mv = sb("mv", [P, RING, 2])
        gate = sb("gate", [P, 1])
        power = sb("power", [P, 1])
        veps = sb("veps", [P, RING])
        rstd = sb("rstd", [P, RING])
        nmr = sb("nmr", [P, RING])
        h_t = sb("h_t", [P, 2, D])
        hT = sb("hT", [P, 2, D])

        x_loaded = [sem(f"x_loaded{b}") for b in range(RING)]
        wseq_loaded, a_loaded = sem("wseq_loaded"), sem("a_loaded")
        w2_loaded = sem("w2_loaded")
        id_set, const_ready = sem("id_set"), sem("const_ready")
        wa_ready = sem("wa_ready")
        var_ready, rstd_ready = sem("var_ready"), sem("rstd_ready")
        ln_ready, h_done, tr_done, hT_done, mm_done, seq_copied = (
            sem(s) for s in ("ln_ready", "h_done", "tr_done", "hT_done", "mm_done", "seq_copied"))
        dve_step = sem("dve_step")
        setup_mm, setup_copied = sem("setup_mm"), sem("setup_copied")

        first = ctx.enter_context(ExitStack())
        x_ring = sb("x_ring", [P, RING, D], stack=first)
        w_q = sb("w_q", [P, C, D], stack=first)
        w_k = sb("w_k", [P, C, D], stack=first)
        w_v = sb("w_v", [P, C, D], stack=first)
        wa_tmp = sb("wa_tmp", [P, C, D], stack=first)

        block = nc.Block()
        with block:
            @block.sync
            def _(sp):
                for b in range(RING):
                    sp.dma_start(x_ring[:, b, :], x[b * P:(b + 1) * P, :]).then_inc(x_loaded[b], 16)
                with sp.Fori(1, T // RING) as g:
                    for b in range(RING):
                        sp.wait_ge(h_done, g * RING - RING + b + 1)
                        sp.dma_start(x_ring[:, b, :], x[bass.ds(g * (RING * P) + b * P, P), :]).then_inc(x_loaded[b], 16)

            @block.gpsimd
            def _(pool):
                pool.memset(ones[:, :], 1.0).then_inc(const_ready, 1)
                pool.memset(ident[:, :], 0.0).then_inc(id_set, 1)
                pool.wait_ge(id_set, 1)
                pool.affine_select(out=ident[:, :], in_=ident[:, :], compare_op=ALU.not_equal, fill=1.0,
                                   base=0, pattern=[[-1, P]], channel_multiplier=1).then_inc(const_ready, 1)
                pool.memset(power[:, :], -0.5).then_inc(id_set, 1)
                pool.wait_ge(id_set, 2)
                with pool.Fori(0, T // RING) as g:
                    for b in range(RING):
                        pool.wait_ge(var_ready, g * RING + b + 1)
                        pool.tensor_tensor(rstd[:, b:b + 1], veps[:, b:b + 1], power[:, :], ALU.pow).then_inc(rstd_ready, 1)

            @block.scalar
            def _(act):
                act.dma_start(w_seq[:, :, :], w_seq_d.rearrange("(c p) n -> p c n", p=P)).then_inc(wseq_loaded, 16)
                act.dma_start(a_bc[:, 0, :], a2_d.partition_broadcast(P)).then_inc(a_loaded, 16)
                act.dma_start(a_bc[:, 1, :], a1_d.partition_broadcast(P)).then_inc(a_loaded, 16)
                for w, d in ((w_q, wq_d), (w_k, wk_d)):
                    act.dma_start(w[:, :, :], d.rearrange("(p c) n -> p c n", c=C)).then_inc(w2_loaded, 16)
                for w, d in ((w_v, wv_d), (w_out, w_out_d)):
                    act.dma_start(w[:, :, :], d.rearrange("(c p) n -> p c n", p=P)).then_inc(w2_loaded, 16)
                act.dma_start(bout_bc[:, :], b_out_d.partition_broadcast(P)).then_inc(w2_loaded, 16)
                act.dma_start(bv_bc[:, :], bv_d.partition_broadcast(P)).then_inc(w2_loaded, 16)
                act.dma_start(bq_col[:, :], bq_d.rearrange("(p c) -> p c", c=C)).then_inc(w2_loaded, 16)
                act.dma_start(bk_col[:, :], bk_d.rearrange("(p c) -> p c", c=C)).then_inc(w2_loaded, 16)

                def norm(t, b):
                    act.wait_ge(ln_ready, t + 1)
                    if not (isinstance(t, int) and t < 2):
                        act.wait_ge(tr_done, t - 1)
                    act.activation(h_t[:, b % 2, :], x_ring[:, b, :], ACT.Relu, bias=nmr[:, b:b + 1],
                                   scale=rstd[:, b:b + 1]).then_inc(h_done, 1)

                def copy_hT(t, b):
                    act.wait_ge(tr_done, t + 1)
                    if not (isinstance(t, int) and t < 2):
                        act.wait_ge(mm_done, t - 1)
                    act.activation(hT[:, b % 2, :], bank[b % 2][:, :], ACT.Copy).then_inc(hT_done, 1)

                def copy_seq(t, b):
                    act.wait_ge(mm_done, t + 1)
                    act.activation(seq_all[:, t, 0:D] if isinstance(t, int) else seq_all[:, bass.ds(t, 1), 0:D].rearrange("p a n -> p (a n)"),
                                   bank[2 + b % 2][:, :], ACT.Copy)
                    act.activation(seq_all[:, t, D:SX] if isinstance(t, int) else seq_all[:, bass.ds(t, 1), D:SX].rearrange("p a n -> p (a n)"),
                                   bank[4 + b % 2][:, 0:2 * H], ACT.Copy).then_inc(seq_copied, 1)

                norm(0, 0)
                copy_hT(0, 0)
                for t in range(1, RING + 1):
                    norm(t, t % RING)
                    copy_hT(t, t % RING)
                    copy_seq(t - 1, (t - 1) % RING)
                with act.Fori(1, T // RING - 1) as g:
                    for b in range(RING):
                        t = g * RING + b + 1
                        norm(t, (b + 1) % RING)
                        copy_hT(t, (b + 1) % RING)
                        copy_seq(g * RING + b, b)
                for t in range(T - RING + 1, T):
                    norm(t, t % RING)
                    copy_hT(t, t % RING)
                    copy_seq(t - 1, (t - 1) % RING)
                copy_seq(T - 1, (T - 1) % RING)

            @block.vector
            def _(dve):
                n = [0]

                def step(ins):
                    n[0] += 1
                    ins.then_inc(dve_step, 1)
                    dve.wait_ge(dve_step, n[0])

                dve.wait_ge(wseq_loaded, 16)
                dve.wait_ge(a_loaded, 32)
                for k in range(2):
                    step(dve.tensor_tensor(
                        wa_tmp[:, :, :].rearrange("p c (h d) -> p (c h) d", d=DH),
                        w_seq[:, :, :].rearrange("p c (h d) -> p (c h) d", d=DH),
                        a_bc[:, k, :].unsqueeze(1).to_broadcast([P, C * H, DH]), ALU.mult))
                    red = dve.tensor_reduce(w_a[:, :, k * H:(k + 1) * H],
                                            wa_tmp[:, :, :].rearrange("p c (h d) -> p c h d", d=DH), AX_X, ALU.add)
                    if k == 0:
                        step(red)
                    else:
                        red.then_inc(wa_ready, 1)
                base = n[0]
                per_tile = 2

                def ln(t, b, first_use):
                    at = base + t * per_tile
                    dve.wait_ge(x_loaded[b], (16 if first_use else 16 * (t // RING + 1)) if isinstance(t, int) else (t - b) * (16 // RING) + 16)
                    if not first_use:
                        dve.wait_ge(h_done, t - RING + 1)
                    dve.bn_stats(stats[:, b, :], x_ring[:, b, :]).then_inc(dve_step, 1)
                    dve.wait_ge(dve_step, at + 1)
                    dve.memset(gate[:, :], 0.0)
                    dve.bn_aggr(mv[:, b, :], stats[:, b, :]).then_inc(dve_step, 1)
                    dve.wait_ge(dve_step, at + 2)
                    dve.tensor_scalar(veps[:, b:b + 1], mv[:, b, 1:2], EPS, None, ALU.add).then_inc(var_ready, 1)
                    dve.wait_ge(rstd_ready, t + 1)
                    dve.scalar_tensor_tensor(nmr[:, b:b + 1], mv[:, b, 0:1], -1.0, rstd[:, b:b + 1],
                                             ALU.mult, ALU.mult).then_inc(ln_ready, 1)

                for b in range(RING):
                    ln(b, b, True)
                with dve.Fori(1, T // RING) as g:
                    for b in range(RING):
                        ln(g * RING + b, b, False)

            @block.tensor
            def _(pe):
                def transposes(t, b):
                    pe.wait_ge(h_done, t + 1)
                    if not (isinstance(t, int) and t < 2):
                        pe.wait_ge(hT_done, t - 1)
                    for c in range(C):
                        last = pe.transpose(bank[b % 2][:, c * P:(c + 1) * P], h_t[:, b % 2, c * P:(c + 1) * P], ident[:, :])
                    last.then_inc(tr_done, 1)

                def products(t, b):
                    pe.wait_ge(hT_done, t + 1)
                    if not (isinstance(t, int) and t < 2):
                        pe.wait_ge(seq_copied, t - 1)
                    for c in range(C):
                        pe.matmul(bank[2 + b % 2][:, :], hT[:, b % 2, c * P:(c + 1) * P], w_seq[:, c, :],
                                  start=(c == 0), stop=(c == C - 1))
                    for c in range(C):
                        last = pe.matmul(bank[4 + b % 2][:, 0:2 * H], hT[:, b % 2, c * P:(c + 1) * P], w_a[:, c, :],
                                         start=(c == 0), stop=(c == C - 1))
                    last.then_inc(mm_done, 1)

                pe.wait_ge(const_ready, 2)
                pe.wait_ge(wa_ready, 1)
                transposes(0, 0)
                for t in range(1, RING + 1):
                    transposes(t, t % RING)
                    products(t - 1, (t - 1) % RING)
                with pe.Fori(1, T // RING - 1) as g:
                    for b in range(RING):
                        transposes(g * RING + b + 1, (b + 1) % RING)
                        products(g * RING + b, b)
                for t in range(T - RING + 1, T):
                    transposes(t, t % RING)
                    products(t - 1, (t - 1) % RING)
                products(T - 1, (T - 1) % RING)

        block = nc.Block()
        with block:
            @block.tensor
            def _(pe):
                pe.wait_ge(w2_loaded, 8 * 16)
                for m in range(C):
                    for c in range(C):
                        last = pe.matmul(bank[m][:, :], w_q[:, c, m * P:(m + 1) * P], w_k[:, c, :],
                                         start=(c == 0), stop=(c == C - 1))
                last.then_inc(setup_mm, 1)
                for m in range(C):
                    for c in range(C):
                        last = pe.transpose(bank[4 + m % 2][:, c * P:(c + 1) * P], w_v[:, c, m * P:(m + 1) * P], ident[:, :])
                    last.then_inc(setup_mm, 1)
                    if m >= 1:
                        pe.wait_ge(setup_copied, m)
                for m in range(C):
                    for c in range(C):
                        pe.matmul(bank[6][:, m:m + 1], w_k[:, c, m * P:(m + 1) * P], bq_col[:, c:c + 1],
                                  start=(c == 0), stop=(c == C - 1))
                for m in range(C):
                    for c in range(C):
                        pe.matmul(bank[6][:, C + m:C + m + 1], w_q[:, c, m * P:(m + 1) * P], bk_col[:, c:c + 1],
                                  start=(c == 0), stop=(c == C - 1))
                for c in range(C):
                    last = pe.matmul(bank[6][0:1, 2 * C:2 * C + 1], bq_col[:, c:c + 1], bk_col[:, c:c + 1],
                                     start=(c == 0), stop=(c == C - 1))
                last.then_inc(setup_mm, 1)

            @block.scalar
            def _(act):
                act.wait_ge(setup_mm, 2)
                for m in range(C):
                    act.wait_ge(setup_mm, 2 + m)
                    act.activation(wv_t[:, m, :], bank[4 + m % 2][:, :], ACT.Copy).then_inc(setup_copied, 1)

            @block.vector
            def _(dve):
                dve.wait_ge(setup_mm, 1)
                for m in range(C):
                    dve.tensor_copy(w_qk[:, m, :], bank[m][:, :])
                dve.wait_ge(setup_mm, 2 + C)
                dve.tensor_copy(u_bias[:, :], bank[6][:, 0:C])
                dve.tensor_copy(c_vec[:, :], bank[6][:, C:2 * C])
                dve.tensor_copy(bqk[:, :], bank[6][0:1, 2 * C:2 * C + 1])
        first.close()
        dense_layers(nc, dict(locals()))


def dense_layers(nc, v):
    ctx = ExitStack()
    (x, adj, out, bank, ident, ones, seq_all, w_out, w_qk, wv_t, bout_bc, bv_bc, u_bias, c_vec, bqk, s2t_dram,
     h_t, hT) = (v[k] for k in (
        "x adj out bank ident ones seq_all w_out w_qk wv_t bout_bc bv_bc u_bias c_vec bqk s2t_dram h_t hT").split())
    with ctx:
        def sb(name, shape, dt=F32):
            return ctx.enter_context(nc.sbuf_tensor(name, shape, dt))

        def sem(name):
            return ctx.enter_context(nc.semaphore("dense_" + name))

        h1 = sb("d_h1", [P, T, D])
        h1T = sb("d_h1T", [P, C, N])
        adj_t = sb("d_adj", [P, N])
        s2_bc = sb("d_s2", [P, N])
        z = sb("d_z", [P, N])
        s2t = s2_bc
        eT = sb("d_eT", [P, N])
        eT2 = eT
        hid, xt, y, e = sb("d_hid", [P, D]), sb("d_x", [P, D]), sb("d_y", [P, D]), sb("d_e", [P, D])
        uT = sb("d_uT", [P, C, P])
        cT = sb("d_cT", [1, P])
        small = sb("d_small", [P, 8])
        st6 = sb("d_st6", [P, 6])
        mv2 = sb("d_mv2", [P, 2])
        x1_dram = nc.dram_tensor("x1_dram", [N, D], F32, kind="Internal").ap()

        s2_tr, s2_copied, s2_stored = sem("s2_tr"), sem("s2_copied"), sem("s2_stored")
        adj_loaded, x_loaded, s2_loaded = sem("adj_loaded"), sem("x_loaded"), sem("s2_loaded")
        pen_ready, score_ready, exp_done, tr_done, eT_done, pv_done, head_done = (
            sem(s) for s in "pen_ready score_ready exp_done tr_done eT_done pv_done head_done".split())
        hidT_tr, hidT_done, proj_done, y_ready, elu_exp, ln_ready, h1_done, h1_tr, h1T_done, x1_stored, x1_ready = (
            sem(s) for s in "hidT_tr hidT_done proj_done y_ready elu_exp ln_ready h1_done h1_tr h1T_done x1_stored x1_ready".split())
        dve_step = sem("dve_step")
        var_ready, rstd_ready = sem("var_ready"), sem("rstd_ready")
        tail_step, l1_step, out_stored = sem("tail_step"), sem("l1_step"), sem("out_stored")
        adj2_loaded, x2_loaded = sem("adj2_loaded"), sem("x2_loaded")
        u_done, u_copied, z_done, z_ready, p_done, p_tr, pT_done, agg_done, agg_ready, aT_tr, aT_done, o_done, o_ready = (
            sem(s) for s in "u_done u_copied z_done z_ready p_done p_tr pT_done agg_done agg_ready aT_tr aT_done o_done o_ready".split())

        def col(ap, t, lo, hi):
            return ap[:, bass.ds(t, 1), lo:hi].rearrange("p a n -> p (a n)")

        block = nc.Block()
        with block:
            @block.tensor
            def _(pe):
                for t in range(T):
                    last = pe.transpose(bank[t // 4][0:H, (t % 4) * P:(t % 4 + 1) * P], seq_all[:, t, D:D + H], ident[:, :])
                last.then_inc(s2_tr, 1)

            @block.vector
            def _(dve):
                dve.wait_ge(s2_tr, 1)
                for k in range(4):
                    last = dve.tensor_copy(s2t[0:H, k * 512:(k + 1) * 512], bank[k][0:H, :])
                    last.then_inc(s2_copied, 1)

            @block.sync
            def _(sp):
                sp.wait_ge(s2_copied, 4)
                sp.dma_start(s2t_dram, s2t[0:H, :]).then_inc(s2_stored, 16)
                sp.wait_ge(s2_stored, 16)

        block = nc.Block()
        with block:
            @block.gpsimd
            def _(pool):
                with pool.Fori(0, T) as t:
                    pool.wait_ge(var_ready, t + 1)
                    pool.tensor_tensor(small[:, 3:4], small[:, 5:6], v["power"][:, :], ALU.pow).then_inc(rstd_ready, 1)

            @block.sync
            def _(sp):
                with sp.Fori(0, T) as t:
                    sp.dma_start(adj_t[:, :], adj[bass.ds(t * P, P), :]).then_inc(adj_loaded, 16)
                    sp.dma_start(xt[:, :], x[bass.ds(t * P, P), :]).then_inc(x_loaded, 16)
                    with sp.Fori(0, H) as h:
                        k = t * H + h
                        sp.wait_ge(pv_done, k + 1)
                        sp.dma_start(s2_bc[:, :], s2t_dram[bass.ds(h, 1), :].rearrange("a n -> (a n)").partition_broadcast(P)).then_inc(s2_loaded, 16)
                    sp.wait_ge(h1_done, t + 1)
                    sp.dma_start(x1_dram[bass.ds(t * P, P), :], y[:, :]).then_inc(x1_stored, 16)
                    sp.wait_ge(x1_stored, t * 16 + 16)
                    sp.sem_inc(x1_ready, 1)
                sp.wait_ge(x1_stored, T * 16)

            def dve_tail(dve, t):
                at = t * 6
                dve.wait_ge(proj_done, t + 1)
                dve.wait_ge(x_loaded, t * 16 + 16)
                dve.tensor_tensor(y[:, :], bank[4][:, :], bout_bc[:, :], ALU.add).then_inc(tail_step, 1)
                dve.wait_ge(tail_step, at + 1)
                dve.tensor_scalar(e[:, :], y[:, :], 0.0, None, ALU.min).then_inc(y_ready, 1)
                dve.scalar_tensor_tensor(y[:, :], y[:, :], 0.0, xt[:, :], ALU.max, ALU.add).then_inc(tail_step, 1)
                dve.wait_ge(tail_step, at + 2)
                dve.wait_ge(elu_exp, t + 1)
                dve.scalar_tensor_tensor(y[:, :], e[:, :], -1.0, y[:, :], ALU.add, ALU.add).then_inc(tail_step, 1)
                dve.wait_ge(tail_step, at + 3)
                dve.bn_stats(st6[:, :], y[:, :]).then_inc(tail_step, 1)
                dve.wait_ge(tail_step, at + 4)
                dve.memset(v["gate"][:, :], 0.0)
                dve.bn_aggr(mv2[:, :], st6[:, :]).then_inc(tail_step, 1)
                dve.wait_ge(tail_step, at + 5)
                dve.tensor_scalar(small[:, 5:6], mv2[:, 1:2], EPS, None, ALU.add).then_inc(var_ready, 1)
                dve.wait_ge(rstd_ready, t + 1)
                dve.scalar_tensor_tensor(small[:, 4:5], mv2[:, 0:1], -1.0, small[:, 3:4], ALU.mult, ALU.mult).then_inc(ln_ready, 1)
                dve.wait_ge(h1_done, t + 1)
                dve.tensor_copy(col(h1, t, 0, D), h_t[:, 0, :]).then_inc(tail_step, 1)
                dve.wait_ge(tail_step, at + 6)

            @block.vector
            def _(dve):
                with dve.Fori(0, T) as t:
                    dve.wait_ge(adj_loaded, t * 16 + 16)
                    dve.tensor_scalar(adj_t[:, :], adj_t[:, :], 1.0, MASK, ALU.subtract, ALU.mult).then_inc(pen_ready, 1)
                    dve.wait_ge(pen_ready, t + 1)
                    dve.memset(v["gate"][:, :], 0.0)
                    with dve.Fori(0, H) as h:
                        k = t * H + h
                        at = k * 3
                        dve.wait_ge(s2_loaded, k * 16 + 16)
                        dve.tensor_scalar(s2_bc[:, :], s2_bc[:, :], seq_all[:, :, :].rearrange("p t n -> p (t n)")[:, bass.ds(t * SX + h + (D + H), 1)],
                                          None, ALU.add).then_inc(dve_step, 1)
                        dve.wait_ge(dve_step, at + 1)
                        dve.scalar_tensor_tensor(z[:, :], s2_bc[:, :], ALPHA, s2_bc[:, :], ALU.mult, ALU.max).then_inc(dve_step, 1)
                        dve.wait_ge(dve_step, at + 2)
                        dve.tensor_tensor(z[:, :], z[:, :], adj_t[:, :], ALU.add).then_inc(dve_step, 1)
                        dve.wait_ge(dve_step, at + 3)
                        dve.tensor_reduce(small[:, 0:1], z[:, :], AX_X, ALU.max, negate=True).then_inc(score_ready, 1)
                        for q in range(4):
                            dve.wait_ge(tr_done, k * 4 + q + 1)
                            dve.tensor_copy(eT[:, q * 512:(q + 1) * 512], bank[q % 2][:, :]).then_inc(eT_done, 1)
                        dve.wait_ge(exp_done, k + 1)
                        dve.reciprocal(small[:, 2:3], small[:, 1:2]).then_inc(head_done, 1)
                        dve.wait_ge(head_done, k * 2 + 1)
                        dve.wait_ge(pv_done, k + 2)
                        dve.tensor_scalar(hid[:, bass.ds(h * DH, DH)], bank[2][:, 0:DH], small[:, 2:3], None, ALU.mult).then_inc(head_done, 1)
                        dve.wait_ge(head_done, k * 2 + 2)
                    dve_tail(dve, t)

            @block.scalar
            def _(act):
                with act.Fori(0, T) as t:
                    with act.Fori(0, H) as h:
                        k = t * H + h
                        act.wait_ge(score_ready, k + 1)
                        act.activation(z[:, :], z[:, :], ACT.Exp, bias=small[:, 0:1], accum_out=small[:, 1:2]).then_inc(exp_done, 1)
                    act.wait_ge(hidT_tr, t + 1)
                    act.activation(hT[:, 0, :], bank[3][:, :], ACT.Copy).then_inc(hidT_done, 1)
                    act.wait_ge(y_ready, t + 1)
                    act.activation(e[:, :], e[:, :], ACT.Exp).then_inc(elu_exp, 1)
                    act.wait_ge(ln_ready, t + 1)
                    act.activation(h_t[:, 0, :], y[:, :], ACT.Relu, bias=small[:, 4:5], scale=small[:, 3:4]).then_inc(h1_done, 1)
                    act.wait_ge(h1_tr, t + 1)
                    act.activation(h1T[:, :, bass.ds(t * P, P)],
                                   bank[5][:, :].rearrange("p (c n) -> p c n", c=C), ACT.Copy).then_inc(h1T_done, 1)

            @block.tensor
            def _(pe):
                pe.transpose(bank[2][:, 0:P], ident[:, :], ident[:, :]).then_inc(pv_done, 1)
                with pe.Fori(0, T) as t:
                    with pe.Fori(0, H) as h:
                        k = t * H + h
                        pe.wait_ge(exp_done, k + 1)
                        for q in range(4):
                            if q >= 2:
                                pe.wait_ge(eT_done, k * 4 + q - 1)
                            for i in range(4):
                                j = q * 4 + i
                                last = pe.transpose(bank[q % 2][:, i * P:(i + 1) * P], z[:, j * P:(j + 1) * P], ident[:, :])
                            last.then_inc(tr_done, 1)
                        pe.wait_ge(eT_done, k * 4 + 4)
                        for j in range(T):
                            last = pe.matmul(bank[2][:, 0:DH], eT[:, j * P:(j + 1) * P],
                                             seq_all[:, j, :][:, bass.ds(h * DH, DH)], start=(j == 0), stop=(j == T - 1))
                        last.then_inc(pv_done, 1)
                    pe.wait_ge(head_done, (t + 1) * (2 * H))
                    for c in range(C):
                        last = pe.transpose(bank[3][:, c * P:(c + 1) * P], hid[:, c * P:(c + 1) * P], ident[:, :])
                    last.then_inc(hidT_tr, 1)
                    pe.wait_ge(hidT_done, t + 1)
                    for c in range(C):
                        last = pe.matmul(bank[4][:, :], hT[:, 0, c * P:(c + 1) * P], w_out[:, c, :],
                                         start=(c == 0), stop=(c == C - 1))
                    last.then_inc(proj_done, 1)
                    pe.wait_ge(h1_done, t + 1)
                    for c in range(C):
                        last = pe.transpose(bank[5][:, c * P:(c + 1) * P], h_t[:, 0, c * P:(c + 1) * P], ident[:, :])
                    last.then_inc(h1_tr, 1)
                    pe.wait_ge(h1T_done, t + 1)

        block = nc.Block()
        with block:
            @block.sync
            def _(sp):
                with sp.Fori(0, T) as t:
                    sp.wait_ge(o_ready, t + 1)
                    sp.dma_start(adj_t[:, :], adj[bass.ds(t * P, P), :]).then_inc(adj2_loaded, 16)
                    sp.dma_start(xt[:, :], x1_dram[bass.ds(t * P, P), :]).then_inc(x2_loaded, 16)
                    sp.wait_ge(o_ready, t + 2)
                    sp.dma_start(out[bass.ds(t * P, P), :], y[:, :]).then_inc(out_stored, 16)
                sp.wait_ge(out_stored, T * 16)

            @block.vector
            def _(dve):
                dve.memset(small[:, 7:8], 0.0).then_inc(o_ready, 1)
                with dve.Fori(0, T) as t:
                    at = t * 9
                    dve.wait_ge(adj2_loaded, t * 16 + 16)
                    for q in range(4):
                        dve.wait_ge(z_done, t * 4 + q + 1)
                        dve.scalar_tensor_tensor(z[:, q * 512:(q + 1) * 512], bank[q][:, :], SCALE,
                                                 adj_t[:, q * 512:(q + 1) * 512], ALU.mult, ALU.mult).then_inc(l1_step, 1)
                    dve.wait_ge(l1_step, at + 4)
                    dve.tensor_scalar(s2_bc[:, :], z[:, :], 0.0, -10000.0, ALU.is_equal, ALU.mult).then_inc(l1_step, 1)
                    dve.wait_ge(l1_step, at + 5)
                    dve.tensor_tensor(z[:, :], z[:, :], s2_bc[:, :], ALU.add).then_inc(l1_step, 1)
                    dve.wait_ge(l1_step, at + 6)
                    dve.tensor_reduce(small[:, 0:1], z[:, :], AX_X, ALU.max, negate=True).then_inc(z_ready, 1)
                    for q in range(4):
                        dve.wait_ge(p_tr, t * 4 + q + 1)
                        dve.tensor_copy(eT2[:, q * 512:(q + 1) * 512], bank[q % 2][:, :]).then_inc(pT_done, 1)
                    dve.wait_ge(p_done, t + 1)
                    dve.reciprocal(small[:, 2:3], small[:, 1:2]).then_inc(l1_step, 1)
                    dve.wait_ge(l1_step, at + 7)
                    dve.wait_ge(agg_done, t + 1)
                    dve.tensor_scalar(hid[:, :], bank[4][:, :], small[:, 2:3], None, ALU.mult).then_inc(agg_ready, 1)
                    dve.wait_ge(o_done, t + 1)
                    dve.tensor_tensor(e[:, :], bank[6][:, :], bv_bc[:, :], ALU.add).then_inc(l1_step, 1)
                    dve.wait_ge(l1_step, at + 8)
                    dve.wait_ge(x2_loaded, t * 16 + 16)
                    dve.scalar_tensor_tensor(y[:, :], e[:, :], 0.0, xt[:, :], ALU.max, ALU.add).then_inc(l1_step, 1)
                    dve.wait_ge(l1_step, at + 9)
                    dve.wait_ge(agg_ready, t + 1)
                    dve.memset(small[:, 7:8], 0.0).then_inc(o_ready, 1)
                    dve.wait_ge(out_stored, t * 16 + 16)

            @block.scalar
            def _(act):
                with act.Fori(0, T) as t:
                    act.wait_ge(u_done, t + 1)
                    for m in range(C):
                        act.activation(uT[:, m, :], bank[5][:, m * P:(m + 1) * P], ACT.Identity, bias=u_bias[:, m:m + 1])
                    act.activation(cT[:, :], bank[7][0:1, 0:P], ACT.Identity, bias=bqk[:, :]).then_inc(u_copied, 1)
                    act.wait_ge(z_ready, t + 1)
                    act.activation(z[:, :], z[:, :], ACT.Exp, bias=small[:, 0:1], accum_out=small[:, 1:2]).then_inc(p_done, 1)
                    act.wait_ge(aT_tr, t + 1)
                    act.activation(hT[:, 0, :], bank[5][:, :], ACT.Copy).then_inc(aT_done, 1)

            @block.tensor
            def _(pe):
                with pe.Fori(0, T) as t:
                    for m in range(C):
                        for c in range(C):
                            pe.matmul(bank[5][:, m * P:(m + 1) * P], w_qk[:, c, m * P:(m + 1) * P],
                                      h1T[:, c, :][:, bass.ds(t * P, P)], start=(c == 0), stop=(c == C - 1))
                    for c in range(C):
                        last = pe.matmul(bank[7][0:1, 0:P], c_vec[:, c:c + 1], h1T[:, c, :][:, bass.ds(t * P, P)],
                                         start=(c == 0), stop=(c == C - 1))
                    last.then_inc(u_done, 1)
                    pe.wait_ge(u_copied, t + 1)
                    for q in range(4):
                        for c in range(C):
                            pe.matmul(bank[q][:, :], uT[:, c, :], h1T[:, c, q * 512:(q + 1) * 512], start=(c == 0), stop=False)
                        pe.matmul(bank[q][:, :], cT[:, :], ones[0:1, :], start=False, stop=True).then_inc(z_done, 1)
                    pe.wait_ge(p_done, t + 1)
                    for q in range(4):
                        if q >= 2:
                            pe.wait_ge(pT_done, t * 4 + q - 1)
                        for i in range(4):
                            j = q * 4 + i
                            last = pe.transpose(bank[q % 2][:, i * P:(i + 1) * P], z[:, j * P:(j + 1) * P], ident[:, :])
                        last.then_inc(p_tr, 1)
                    pe.wait_ge(pT_done, t * 4 + 4)
                    for j in range(T):
                        last = pe.matmul(bank[4][:, :], eT2[:, j * P:(j + 1) * P], h1[:, j, :], start=(j == 0), stop=(j == T - 1))
                    last.then_inc(agg_done, 1)
                    pe.wait_ge(agg_ready, t + 1)
                    for c in range(C):
                        last = pe.transpose(bank[5][:, c * P:(c + 1) * P], hid[:, c * P:(c + 1) * P], ident[:, :])
                    last.then_inc(aT_tr, 1)
                    pe.wait_ge(aT_done, t + 1)
                    for c in range(C):
                        last = pe.matmul(bank[6][:, :], hT[:, 0, c * P:(c + 1) * P], wv_t[:, c, :],
                                         start=(c == 0), stop=(c == C - 1))
                    last.then_inc(o_done, 1)
                    pe.wait_ge(o_ready, t + 2)


_INS = ["x", "adj", "L0_gnn_W_seq", "L0_gnn_a1", "L0_gnn_a2", "L0_gnn_W_out", "L0_gnn_b_out", "L1_gnn_W_q",
        "L1_gnn_b_q", "L1_gnn_W_k", "L1_gnn_b_k", "L1_gnn_W_v", "L1_gnn_b_v"]


def kernel(**inputs):
    import numpy as _np
    import concourse.bacc as _bacc
    from concourse import mybir as _mybir
    from concourse.bass_utils import run_bass_kernel_spmd as _run

    nc = _bacc.Bacc("TRN2", target_bir_lowering=False, num_devices=1)
    arrays, args = {}, []
    for name in _INS:
        a = _np.ascontiguousarray(inputs[name])
        arrays[f"in_{name}_dram"] = a
        args.append(nc.dram_tensor(f"in_{name}_dram", a.shape, _mybir.dt.from_np(a.dtype), kind="ExternalInput").ap())
    out = nc.dram_tensor("out_0_dram", (N, D), F32, kind="ExternalOutput").ap()
    build(nc, *args, out)
    r = _run(nc, [arrays], core_ids=[0])
    return r.results[0]["out_0_dram"]
```

```python
from contextlib import ExitStack

import concourse.bass as bass
from concourse import mybir

ALU = mybir.AluOpType
ACT = mybir.ActivationFunctionType
AX_X = mybir.AxisListType.X
F32 = mybir.dt.float32
I32 = mybir.dt.int32
U32 = mybir.dt.uint32

P = 128
N = 2048
D = 512
T = N // P
C = D // P
H = 16
DH = D // H
SX = D + 2 * H
EPS = 1e-5
ALPHA = 0.2
MASK = 65500.0
SCALE = float(D) ** -0.5
RING = 4
SG = D + H
TOP = 8

SLOT_TILES = [15, 11, 6, 3, 2, 1, 1, 1]
LONE_RANK = 13 * P

FIRST_TILE = 11
ORDER = [(k + FIRST_TILE) % T for k in range(T)]
SLOTS = [sum(n > t for n in SLOT_TILES) for t in ORDER]
FIRST_SLOT = [sum(SLOTS[:k]) for k in range(T + 1)]
NSLOT = FIRST_SLOT[T]
REUSE = 30
LONE0 = ORDER.index(LONE_RANK // P)
LONE = T - LONE_RANK // P
LN = LONE * P
RUNS = []
for _k in range(T):
    if RUNS and RUNS[-1][2] == SLOTS[_k]:
        RUNS[-1][1] += 1
    else:
        RUNS.append([_k, 1, SLOTS[_k]])
RUNS = [r for r in RUNS if r[2]]
assert all(FIRST_SLOT[r[0]] // REUSE == (FIRST_SLOT[r[0]] + r[1] * r[2] - 1) // REUSE for r in RUNS)
GATHERED = 6
AHEAD = 6
W2 = 2 * (DH + 1)
PAY = TOP + 2 + H
FAR = 1e30
LIMIT = 1e4


def build(nc, x, adj, w_seq_d, a1_d, a2_d, w_out_d, b_out_d, wq_d, bq_d, wk_d, bk_d, wv_d, bv_d, out):
    ctx = ExitStack()
    with ctx:
        def sb(name, shape, dt=F32, stack=ctx):
            return stack.enter_context(nc.sbuf_tensor(name, shape, dt))

        def sem(name):
            return ctx.enter_context(nc.semaphore(name))

        psum = ctx.enter_context(nc.psum_tensor("psum", [P, 8, 512], F32))
        bank = [psum[:, i, :] for i in range(8)]

        s2t_dram = nc.dram_tensor("s2t_dram", [H, N], F32, kind="Internal").ap()

        seq_dram = nc.dram_tensor("seq_dram", [N, SG], F32, kind="Internal").ap()
        record_dram = nc.dram_tensor("record_dram", [N, PAY], U32, kind="Internal").ap()
        h1_dram = nc.dram_tensor("h1_dram", [N, D], F32, kind="Internal").ap()
        s1t_dram = nc.dram_tensor("s1t_dram", [H, LN], F32, kind="Internal").ap()

        ident = sb("ident", [P, P])
        ones = sb("ones", [P, 512])
        w_seq = sb("w_seq", [P, C, D])
        w_out = sb("w_out", [P, C, D])
        w_qk = sb("w_qk", [P, C, D])
        wv_t = sb("wv_t", [P, C, D])
        w_a = sb("w_a", [P, C, 2 * H])
        bout_bc = sb("bout_bc", [P, D])
        bv_bc = sb("bv_bc", [P, D])
        a_bc = sb("a_bc", [P, 2, DH])
        bq_col = sb("bq_col", [P, C])
        bk_col = sb("bk_col", [P, C])
        u_bias = sb("u_bias", [P, C])
        c_vec = sb("c_vec", [P, C])
        bqk = sb("bqk", [P, 1])
        u_bias_bc = sb("u_bias_bc", [P, D])
        near = sb("near", [P, T, 2, TOP])
        square = sb("square", [P, T])
        record = sb("record", [P, T, PAY], U32)
        rank = sb("rank", [P, T], U32)
        s2_max = sb("s2_max", [P, H])
        b_exp = sb("b_exp", [P, T, H])
        d_exp = sb("d_exp", [P, T, H])
        neg_s2 = sb("neg_s2", [P, T, H])
        flag = sb("flag", [1, 1], I32)
        slot_no = sb("slot_no", [P, TOP])
        seq_all = sb("seq_all", [P, T, SX])
        stats = sb("stats", [P, RING, 6])
        mv = sb("mv", [P, RING, 2])
        gate = sb("gate", [P, 1])
        power = sb("power", [P, 1])
        veps = sb("veps", [P, RING])
        rstd = sb("rstd", [P, RING])
        nmr = sb("nmr", [P, RING])
        h_t = sb("h_t", [P, 2, D])
        hT = sb("hT", [P, 2, D])

        x_loaded = [sem(f"x_loaded{b}") for b in range(RING)]
        wseq_loaded, a_loaded = sem("wseq_loaded"), sem("a_loaded")
        w2_loaded = sem("w2_loaded")
        id_set, const_ready = sem("id_set"), sem("const_ready")
        wa_ready = sem("wa_ready")
        var_ready, rstd_ready = sem("var_ready"), sem("rstd_ready")
        ln_ready, h_done, tr_done, hT_done, mm_done, seq_copied = (
            sem(s) for s in ("ln_ready", "h_done", "tr_done", "hT_done", "mm_done", "seq_copied"))
        adj_loaded = [sem(f"adj_loaded{b}") for b in range(RING)]
        adj_squared, adj_searched = sem("adj_squared"), sem("adj_searched")
        seq_stored = sem("seq_stored")
        dve_step = sem("dve_step")
        setup_mm, setup_copied = sem("setup_mm"), sem("setup_copied")

        first = ctx.enter_context(ExitStack())
        x_ring = sb("x_ring", [P, RING, D], stack=first)
        adj_ring = sb("adj_ring", [P, RING, N], stack=first)
        squares = sb("squares", [P, N], mybir.dt.bfloat16, stack=first)
        top_ring = sb("top_ring", [P, 2, TOP], stack=first)
        w_q = sb("w_q", [P, C, D], stack=first)
        w_k = sb("w_k", [P, C, D], stack=first)
        w_v = sb("w_v", [P, C, D], stack=first)
        wa_tmp = sb("wa_tmp", [P, C, D], stack=first)

        block = nc.Block()
        with block:
            @block.sync
            def _(sp):
                for b in range(RING):
                    sp.dma_start(x_ring[:, b, :], x[b * P:(b + 1) * P, :]).then_inc(x_loaded[b], 16)
                    sp.dma_start(adj_ring[:, b, :], adj[b * P:(b + 1) * P, :]).then_inc(adj_loaded[b], 16)
                with sp.Fori(1, T // RING) as g:
                    for b in range(RING):
                        sp.wait_ge(adj_searched, g * RING - RING + b + 1)
                        sp.wait_ge(adj_squared, g * RING - RING + b + 1)
                        sp.dma_start(adj_ring[:, b, :], adj[bass.ds(g * (RING * P) + b * P, P), :]).then_inc(adj_loaded[b], 16)
                        sp.wait_ge(h_done, g * RING - RING + b + 1)
                        sp.dma_start(x_ring[:, b, :], x[bass.ds(g * (RING * P) + b * P, P), :]).then_inc(x_loaded[b], 16)

            @block.gpsimd
            def _(pool):
                pool.memset(ones[:, :], 1.0).then_inc(const_ready, 1)
                pool.memset(ident[:, :], 0.0).then_inc(id_set, 1)
                pool.wait_ge(id_set, 1)
                pool.affine_select(out=ident[:, :], in_=ident[:, :], compare_op=ALU.not_equal, fill=1.0,
                                   base=0, pattern=[[-1, P]], channel_multiplier=1).then_inc(const_ready, 1)
                pool.memset(power[:, :], -0.5).then_inc(id_set, 1)
                pool.wait_ge(id_set, 2)
                pool.iota(slot_no[:, :], pattern=[[1, TOP]], base=0, channel_multiplier=0,
                          allow_small_or_imprecise_dtypes=True).then_inc(id_set, 1)
                for t in range(T):
                    pool.wait_ge(var_ready, t + 1)
                    pool.tensor_tensor(rstd[:, t % RING:t % RING + 1], veps[:, t % RING:t % RING + 1], power[:, :],
                                       ALU.pow).then_inc(rstd_ready, 1)
                    if t >= RING:
                        pool.wait_ge(seq_copied, t - RING + 1)
                        pool.dma_start(seq_dram[(t - RING) * P:(t - RING + 1) * P, :], seq_all[:, t - RING, 0:SG]).then_inc(seq_stored, 16)
                for t in range(T - RING, T):
                    pool.wait_ge(seq_copied, t + 1)
                    pool.dma_start(seq_dram[t * P:(t + 1) * P, :], seq_all[:, t, 0:SG]).then_inc(seq_stored, 16)
                pool.wait_ge(seq_stored, T * 16)

            @block.scalar
            def _(act):
                act.dma_start(w_seq[:, :, :], w_seq_d.rearrange("(c p) n -> p c n", p=P)).then_inc(wseq_loaded, 16)
                act.dma_start(a_bc[:, 0, :], a2_d.partition_broadcast(P)).then_inc(a_loaded, 16)
                act.dma_start(a_bc[:, 1, :], a1_d.partition_broadcast(P)).then_inc(a_loaded, 16)
                for w, d in ((w_q, wq_d), (w_k, wk_d)):
                    act.dma_start(w[:, :, :], d.rearrange("(p c) n -> p c n", c=C)).then_inc(w2_loaded, 16)
                for w, d in ((w_v, wv_d), (w_out, w_out_d)):
                    act.dma_start(w[:, :, :], d.rearrange("(c p) n -> p c n", p=P)).then_inc(w2_loaded, 16)
                act.dma_start(bout_bc[:, :], b_out_d.partition_broadcast(P)).then_inc(w2_loaded, 16)
                act.dma_start(bv_bc[:, :], bv_d.partition_broadcast(P)).then_inc(w2_loaded, 16)
                act.dma_start(bq_col[:, :], bq_d.rearrange("(p c) -> p c", c=C)).then_inc(w2_loaded, 16)
                act.dma_start(bk_col[:, :], bk_d.rearrange("(p c) -> p c", c=C)).then_inc(w2_loaded, 16)

                def norm(t, b):
                    act.wait_ge(ln_ready, t + 1)
                    if not (isinstance(t, int) and t < 2):
                        act.wait_ge(tr_done, t - 1)
                    act.activation(h_t[:, b % 2, :], x_ring[:, b, :], ACT.Relu, bias=nmr[:, b:b + 1],
                                   scale=rstd[:, b:b + 1]).then_inc(h_done, 1)

                def squares_of(t, b):
                    act.wait_ge(adj_loaded[b], 16 * (t // RING + 1))
                    act.activation(squares[:, :], adj_ring[:, b, :], ACT.Square,
                                   accum_out=square[:, t:t + 1]).then_inc(adj_squared, 1)

                def copy_hT(t, b):
                    act.wait_ge(tr_done, t + 1)
                    if not (isinstance(t, int) and t < 2):
                        act.wait_ge(mm_done, t - 1)
                    act.activation(hT[:, b % 2, :], bank[b % 2][:, :], ACT.Copy).then_inc(hT_done, 1)

                def copy_seq(t, b):
                    act.wait_ge(mm_done, t + 1)
                    act.activation(seq_all[:, t, 0:D],
                                   bank[2 + b % 2][:, :], ACT.Copy)
                    act.activation(seq_all[:, t, D:SX],
                                   bank[4 + b % 2][:, 0:2 * H], ACT.Copy).then_inc(seq_copied, 1)

                norm(0, 0)
                copy_hT(0, 0)
                squares_of(0, 0)
                for t in range(1, T):
                    norm(t, t % RING)
                    copy_hT(t, t % RING)
                    copy_seq(t - 1, (t - 1) % RING)
                    squares_of(t, t % RING)
                copy_seq(T - 1, (T - 1) % RING)

            @block.vector
            def _(dve):
                n = [0]

                def step(ins):
                    n[0] += 1
                    ins.then_inc(dve_step, 1)
                    dve.wait_ge(dve_step, n[0])

                dve.wait_ge(wseq_loaded, 16)
                dve.wait_ge(a_loaded, 32)
                for k in range(2):
                    step(dve.tensor_tensor(
                        wa_tmp[:, :, :].rearrange("p c (h d) -> p (c h) d", d=DH),
                        w_seq[:, :, :].rearrange("p c (h d) -> p (c h) d", d=DH),
                        a_bc[:, k, :].unsqueeze(1).to_broadcast([P, C * H, DH]), ALU.mult))
                    red = dve.tensor_reduce(w_a[:, :, k * H:(k + 1) * H],
                                            wa_tmp[:, :, :].rearrange("p c (h d) -> p c h d", d=DH), AX_X, ALU.add)
                    if k == 0:
                        step(red)
                    else:
                        red.then_inc(wa_ready, 1)

                def ln(t, b):
                    dve.wait_ge(x_loaded[b], 16 * (t // RING + 1))
                    if t >= RING:
                        dve.wait_ge(h_done, t - RING + 1)
                    step(dve.bn_stats(stats[:, b, :], x_ring[:, b, :]))
                    step(dve.bn_aggr(mv[:, b, :], stats[:, b, :]))
                    dve.tensor_scalar(veps[:, b:b + 1], mv[:, b, 1:2], EPS, None, ALU.add).then_inc(var_ready, 1)

                def ln_bias(t, b):
                    dve.wait_ge(rstd_ready, t + 1)
                    dve.scalar_tensor_tensor(nmr[:, b:b + 1], mv[:, b, 0:1], -1.0, rstd[:, b:b + 1],
                                             ALU.mult, ALU.mult).then_inc(ln_ready, 1)

                ln(0, 0)
                ln_bias(0, 0)
                for t in range(T):
                    b = t % RING
                    if t + 1 < T:
                        ln(t + 1, (t + 1) % RING)
                    dve.wait_ge(adj_loaded[b], 16 * (t // RING + 1))
                    step(dve.max(near[:, t, 0, :], adj_ring[:, b, :]))
                    if t + 1 < T:
                        ln_bias(t + 1, (t + 1) % RING)
                    dve.max_index(near[:, t, 1, :].bitcast(U32), near[:, t, 0, :], adj_ring[:, b, :]).then_inc(adj_searched, 1)

            @block.tensor
            def _(pe):
                def transposes(t, b):
                    pe.wait_ge(h_done, t + 1)
                    if not (isinstance(t, int) and t < 2):
                        pe.wait_ge(hT_done, t - 1)
                    for c in range(C):
                        last = pe.transpose(bank[b % 2][:, c * P:(c + 1) * P], h_t[:, b % 2, c * P:(c + 1) * P], ident[:, :])
                    last.then_inc(tr_done, 1)

                def products(t, b):
                    pe.wait_ge(hT_done, t + 1)
                    if not (isinstance(t, int) and t < 2):
                        pe.wait_ge(seq_copied, t - 1)
                    for c in range(C):
                        pe.matmul(bank[2 + b % 2][:, :], hT[:, b % 2, c * P:(c + 1) * P], w_seq[:, c, :],
                                  start=(c == 0), stop=(c == C - 1))
                    for c in range(C):
                        last = pe.matmul(bank[4 + b % 2][:, 0:2 * H], hT[:, b % 2, c * P:(c + 1) * P], w_a[:, c, :],
                                         start=(c == 0), stop=(c == C - 1))
                    last.then_inc(mm_done, 1)

                pe.wait_ge(const_ready, 2)
                pe.wait_ge(wa_ready, 1)
                transposes(0, 0)
                for t in range(1, RING + 1):
                    transposes(t, t % RING)
                    products(t - 1, (t - 1) % RING)
                with pe.Fori(1, T // RING - 1) as g:
                    for b in range(RING):
                        transposes(g * RING + b + 1, (b + 1) % RING)
                        products(g * RING + b, b)
                for t in range(T - RING + 1, T):
                    transposes(t, t % RING)
                    products(t - 1, (t - 1) % RING)
                products(T - 1, (T - 1) % RING)

        s_ctx = ctx.enter_context(ExitStack())
        bq_rep = sb("bq_rep", [P, C, P], stack=s_ctx)
        before = sb("before", [P, P], stack=s_ctx)
        classes = sb("classes", [P, TOP + 1, T], stack=s_ctx)
        hot = sb("hot", [P, TOP + 1, T], stack=s_ctx)
        PADT = 8
        scan = [sb(f"scan{i}", [P, TOP + 1, PADT + T], stack=s_ctx) for i in range(2)]
        above = [sb(f"above{i}", [P, TOP + 1 + 8], stack=s_ctx) for i in range(2)]
        place = sb("place", [P, TOP + 1, T], stack=s_ctx)
        rank_f = sb("rank_f", [P, T], stack=s_ctx)
        deg = sb("deg", [P, T], stack=s_ctx)
        bad = sb("bad", [P, 4], stack=s_ctx)
        tmp = sb("tmp", [P, T, 2 * H], stack=s_ctx)
        caps = sb("caps", [P, TOP], stack=s_ctx)
        max_h = sb("max_h", [P, H], stack=s_ctx)
        max_t = sb("max_t", [H, 1], stack=s_ctx)
        diag = sb("diag", [H, H], stack=s_ctx)
        pool_step, masks_ready = sem("pool_step"), sem("masks_ready")
        hot_ready, rank_mm, max_ready, max_tr, diag_ready, max_mm, bad_ready, bad_mm, rep_ready, prep = (
            sem(k) for k in "hot_ready rank_mm max_ready max_tr diag_ready max_mm bad_ready bad_mm rep_ready prep".split())
        shift_ready, setup_step, act_step = sem("shift_ready"), sem("setup_step"), sem("act_step")
        MASKS = len(SLOT_TILES) + 7
        block = nc.Block()
        with block:
            @block.gpsimd
            def _(pool):
                pool.memset(before[:, :], 0.0).then_inc(pool_step, 1)
                pool.iota(classes[:, :, :], pattern=[[1, TOP + 1], [0, T]], base=0, channel_multiplier=0,
                          allow_small_or_imprecise_dtypes=True).then_inc(masks_ready, 1)
                pool.wait_ge(pool_step, 1)
                pool.affine_select(out=before[:, :], in_=before[:, :], compare_op=ALU.is_ge, fill=1.0,
                                   base=0, pattern=[[-1, P]], channel_multiplier=1).then_inc(masks_ready, 1)
                for s, tiles in enumerate(SLOT_TILES):
                    pool.memset(caps[:, s:s + 1], float(tiles * P)).then_inc(masks_ready, 1)
                for a in scan:
                    pool.memset(a[:, :, :], 0.0).then_inc(masks_ready, 1)
                for a in above:
                    pool.memset(a[:, :], 0.0).then_inc(masks_ready, 1)
                pool.iota(record[:, :, TOP], pattern=[[P, T]], base=0, channel_multiplier=1).then_inc(masks_ready, 1)
            @block.vector
            def _(dve):
                n = [0]

                def step(ins):
                    n[0] += 1
                    ins.then_inc(setup_step, 1)
                    dve.wait_ge(setup_step, n[0])

                values = near[:, :, 0, :]
                dve.wait_ge(masks_ready, MASKS)
                step(dve.tensor_reduce(deg[:, :], values, AX_X, ALU.add))
                dve.tensor_tensor(hot[:, :, :], deg[:, :].unsqueeze(1).to_broadcast([P, TOP + 1, T]),
                                  classes[:, :, :], ALU.is_equal).then_inc(hot_ready, 1)
                dve.tensor_reduce(max_h[:, :], seq_all[:, :, D:D + H].rearrange("p t h -> p h t"), AX_X, ALU.max).then_inc(max_ready, 1)
                step(dve.tensor_tensor(tmp[:, :, 0:TOP], values, values, ALU.mult))
                step(dve.tensor_tensor(tmp[:, :, 0:TOP], tmp[:, :, 0:TOP], values, ALU.not_equal))
                step(dve.tensor_reduce(bad[:, 0:1], tmp[:, :, 0:TOP], mybir.AxisListType.XY, ALU.add))
                step(dve.tensor_tensor(tmp[:, :, 0], square[:, :], deg[:, :], ALU.not_equal))
                step(dve.tensor_reduce(bad[:, 1:2], tmp[:, :, 0], AX_X, ALU.add))
                step(dve.tensor_tensor(tmp[:, :, :], seq_all[:, :, D:SX], seq_all[:, :, D:SX], ALU.mult))
                step(dve.tensor_scalar(tmp[:, :, :], tmp[:, :, :], LIMIT * LIMIT, None, ALU.is_gt))
                step(dve.tensor_reduce(bad[:, 2:3], tmp[:, :, :], mybir.AxisListType.XY, ALU.add))
                dve.wait_ge(rank_mm, 1)
                step(dve.tensor_copy(scan[0][:, :, PADT:], bank[5][:, 0:(TOP + 1) * T].rearrange("p (c t) -> p c t", t=T)))
                for k, d in enumerate((1, 2, 4, 8)):
                    a, b = scan[k % 2], scan[1 - k % 2]
                    step(dve.tensor_tensor(b[:, :, PADT:], a[:, :, PADT:], a[:, :, PADT - d:PADT + T - d], ALU.add))
                step(dve.tensor_copy(above[0][:, 0:TOP + 1], scan[0][:, :, PADT + T - 1]))
                for k, d in enumerate((1, 2, 4, 8)):
                    a, b = above[k % 2], above[1 - k % 2]
                    step(dve.tensor_tensor(b[:, 0:TOP + 1], a[:, 0:TOP + 1], a[:, d:d + TOP + 1], ALU.add))
                more = above[0][:, 1:TOP + 2]
                step(dve.tensor_tensor(tmp[:, 0, 0:TOP], more[:, 0:TOP], caps[:, :], ALU.is_gt))
                step(dve.tensor_scalar(tmp[:, 0, TOP:TOP + 1], more[:, 0:1], float(LONE_RANK), None, ALU.is_lt))
                step(dve.tensor_reduce(bad[:, 3:4], tmp[:, 0, 0:TOP + 1], AX_X, ALU.add))
                step(dve.tensor_reduce(tmp[:, 1, 0:1], bad[:, :], AX_X, ALU.add))
                dve.tensor_copy(bad[:, 0:1], tmp[:, 1, 0:1]).then_inc(bad_ready, 1)
                dve.wait_ge(rank_mm, 2)
                step(dve.tensor_tensor(place[:, :, :], scan[0][:, :, PADT - 1:PADT + T - 1],
                                       bank[6][:, 0:(TOP + 1) * T].rearrange("p (c t) -> p c t", t=T), ALU.add))
                step(dve.tensor_tensor(place[:, :, :], place[:, :, :], more.unsqueeze(2).to_broadcast([P, TOP + 1, T]), ALU.add))
                step(dve.tensor_tensor(place[:, :, :], place[:, :, :], hot[:, :, :], ALU.mult))
                step(dve.tensor_reduce(rank_f[:, :], place[:, :, :].rearrange("p c t -> p t c"), AX_X, ALU.add))
                step(dve.tensor_copy(rank[:, :], rank_f[:, :]))
                step(dve.tensor_copy(record[:, :, 0:TOP], near[:, :, 1, :].bitcast(U32)))
                step(dve.tensor_copy(record[:, :, TOP + 1].bitcast(F32), deg[:, :]))
                step(dve.tensor_copy(record[:, :, TOP + 2:].bitcast(F32), seq_all[:, :, D + H:SX]))
                dve.wait_ge(max_tr, 1)
                step(dve.tensor_reduce(max_t[:, :], bank[7][0:H, 0:P], AX_X, ALU.max))
                dve.tensor_scalar(diag[:, :], ident[0:H, 0:H], max_t[:, :], None, ALU.mult).then_inc(diag_ready, 1)
                dve.wait_ge(bad_mm, 1)
                dve.tensor_scalar(flag[:, :], bank[7][0:1, 128:129], 0.0, None, ALU.is_equal).then_inc(prep, 1)
                dve.wait_ge(max_mm, 1)
                step(dve.tensor_copy(s2_max[:, :], bank[7][:, 256:256 + H]))
                dve.tensor_tensor(b_exp[:, :, :], seq_all[:, :, D:D + H], s2_max[:, :].unsqueeze(1).to_broadcast([P, T, H]),
                                  ALU.subtract).then_inc(shift_ready, 1)
                dve.tensor_scalar(neg_s2[:, :, :], seq_all[:, :, D:D + H], -1.0, None, ALU.mult).then_inc(prep, 1)

            @block.tensor
            def _(pe):
                pe.wait_ge(hot_ready, 1)
                pe.matmul(bank[5][:, 0:(TOP + 1) * T], ones[:, 0:P], hot[:, :, :].rearrange("p c t -> p (c t)")).then_inc(rank_mm, 1)
                pe.wait_ge(masks_ready, 2)
                pe.matmul(bank[6][:, 0:(TOP + 1) * T], before[:, :], hot[:, :, :].rearrange("p c t -> p (c t)")).then_inc(rank_mm, 1)
                pe.wait_ge(max_ready, 1)
                pe.transpose(bank[7][0:H, 0:P], max_h[:, :], ident[:, :]).then_inc(max_tr, 1)
                pe.wait_ge(w2_loaded, 8 * 16)
                for m in range(C):
                    for c in range(C):
                        last = pe.matmul(bank[m][:, :], w_q[:, c, m * P:(m + 1) * P], w_k[:, c, :],
                                         start=(c == 0), stop=(c == C - 1))
                    last.then_inc(setup_mm, 1)
                pe.wait_ge(diag_ready, 1)
                pe.wait_ge(bad_ready, 1)
                pe.matmul(bank[7][:, 128:129], ones[:, 0:P], bad[:, 0:1]).then_inc(bad_mm, 1)
                pe.wait_ge(prep, 1)
                pe.matmul(bank[7][:, 256:256 + H], ones[0:H, 0:P], diag[:, :]).then_inc(max_mm, 1)
                for m in range(C):
                    pe.wait_ge(setup_copied, m + 1)
                    for c in range(C):
                        last = pe.transpose(bank[m][:, c * P:(c + 1) * P], w_v[:, c, m * P:(m + 1) * P], ident[:, :])
                    last.then_inc(setup_mm, 1)
                pe.wait_ge(rep_ready, 1)
                for c in range(C):
                    last = pe.matmul(bank[4][:, :], bq_rep[:, c, :], w_k[:, c, :], start=(c == 0), stop=(c == C - 1))
                last.then_inc(setup_mm, 1)
                pe.wait_ge(prep, 2)
                for m in range(C):
                    for c in range(C):
                        pe.matmul(bank[6][:, m:m + 1], w_k[:, c, m * P:(m + 1) * P], bq_col[:, c:c + 1],
                                  start=(c == 0), stop=(c == C - 1))
                for m in range(C):
                    for c in range(C):
                        pe.matmul(bank[6][:, C + m:C + m + 1], w_q[:, c, m * P:(m + 1) * P], bk_col[:, c:c + 1],
                                  start=(c == 0), stop=(c == C - 1))
                for c in range(C):
                    last = pe.matmul(bank[6][:, 2 * C:2 * C + 1], bq_rep[:, c, :], bk_col[:, c:c + 1],
                                     start=(c == 0), stop=(c == C - 1))
                last.then_inc(setup_mm, 1)

            @block.scalar
            def _(act):
                act.wait_ge(w2_loaded, 8 * 16)
                act.wait_ge(const_ready, 2)
                for c in range(C):
                    last = act.activation(bq_rep[:, c, :], ones[:, 0:P], ACT.Copy, scale=bq_col[:, c:c + 1])
                last.then_inc(rep_ready, 1)
                for m in range(C):
                    act.wait_ge(setup_mm, m + 1)
                    act.activation(w_qk[:, m, :], bank[m], ACT.Copy).then_inc(setup_copied, 1)
                act.wait_ge(shift_ready, 1)
                act.activation(d_exp[:, :, :], b_exp[:, :, :], ACT.Exp, scale=ALPHA).then_inc(act_step, 1)
                act.wait_ge(act_step, 1)
                act.activation(b_exp[:, :, :], b_exp[:, :, :], ACT.Exp)
                for m in range(C):
                    act.wait_ge(setup_mm, C + m + 1)
                    act.activation(wv_t[:, m, :], bank[m], ACT.Copy)
                act.wait_ge(setup_mm, 2 * C + 1)
                act.activation(u_bias_bc[:, :], bank[4], ACT.Copy)
                act.wait_ge(setup_mm, 2 * C + 2)
                act.activation(u_bias[:, :], bank[6][:, 0:C], ACT.Copy)
                act.activation(c_vec[:, :], bank[6][:, C:2 * C], ACT.Copy)
                act.activation(bqk[:, :], bank[6][:, 2 * C:2 * C + 1], ACT.Copy)
        s_ctx.close()
        first.close()
        sparse = nc.values_load(flag[0:1, 0:1], min_val=0, max_val=1)
        with nc.If(sparse == 1):
            sparse_layers(nc, dict(locals()))
        with nc.Else():
            dense_layers(nc, dict(locals()))


def sparse_layers(nc, v):
    ctx = ExitStack()
    (x, out, psum, bank, ident, ones, seq_all, w_out, w_qk, wv_t, bout_bc, bv_bc, u_bias_bc, c_vec, bqk, h_t, hT, power,
     record, rank, s2_max, b_exp, d_exp, neg_s2, slot_no, seq_dram, record_dram, h1_dram, s1t_dram) = (v[k] for k in (
         "x out psum bank ident ones seq_all w_out w_qk wv_t bout_bc bv_bc u_bias_bc c_vec bqk h_t hT power "
         "record rank s2_max b_exp d_exp neg_s2 slot_no seq_dram record_dram h1_dram s1t_dram").split())
    BF16 = mybir.dt.bfloat16
    with ctx:
        def sb(name, shape, dt=F32, stack=ctx):
            return stack.enter_context(nc.sbuf_tensor("s_" + name, shape, dt))

        def sem(name):
            return ctx.enter_context(nc.semaphore("s_" + name))

        def chain(eng, s):
            n = [0]

            def step(ins):
                n[0] += 1
                ins.then_inc(s, 1)
                eng.wait_ge(s, n[0])
            return step

        tab = sb("tab", [P, T, PAY], U32)
        own = tab[:, :, TOP:TOP + 1]
        s1_rank = tab[:, :, TOP + 2:].bitcast(F32)
        degree = tab[:, :, TOP + 1].bitcast(F32)
        x1 = sb("x1", [P, T, D])
        lone = sb("lone", [P, LONE, D])
        valid = sb("valid", [P, T, TOP])
        pen = sb("pen", [P, T, TOP])
        has = sb("has", [P, T])
        has_not = sb("has_not", [P, T])
        others = sb("others", [P, T])
        ones_b = sb("ones_b", [P, P], BF16)
        a_fac = sb("a_fac", [P, LONE, H])
        c_fac = sb("c_fac", [P, LONE, H])

        rec_stored, tab_loaded, x_got = sem("rec_stored"), sem("tab_loaded"), sem("x_got")
        s1_tr, s1_copied, s1_stored, s1_loaded, ones_set = (sem(k) for k in "s1_tr s1_copied s1_stored s1_loaded ones_set".split())
        prep_step, fac_ready = sem("prep_step"), sem("fac_ready")
        lone_ctx = ctx.enter_context(ExitStack())
        s1t = sb("s1t", [H, LN], stack=lone_ctx)
        s1_bc = sb("s1_bc", [P, H, LN], stack=lone_ctx)
        wst = [sb(f"wst{i}", [P, T, W2], stack=lone_ctx) for i in range(2)]
        parts = [sb(f"parts{i}", [P, T, 3, W2], BF16, stack=lone_ctx) for i in range(2)]
        ind = [sb(f"ind{i}", [P, T, LN], BF16, stack=lone_ctx) for i in range(2)]
        s2_col = [sb(f"s2_col{i}", [P, T], stack=lone_ctx) for i in range(2)]
        ev = sb("ev", [P, LONE + 1, W2], stack=lone_ctx)
        bt = sb("bt", [P, LONE, DH + 1], stack=lone_ctx)
        dt_ = sb("dt", [P, LONE, DH + 1], stack=lone_ctx)
        rec = sb("rec", [P, LONE, 1], stack=lone_ctx)

        block = nc.Block()
        with block:
            @block.gpsimd
            def _(pool):
                for t in range(T):
                    pool.indirect_dma_start(record_dram[:, :], bass.IndirectOffsetOnAxis(rank[:, t:t + 1], 0),
                                            record[:, t, :], None).then_inc(rec_stored, 16)
                pool.memset(ones_b[:, :], 1.0).then_inc(ones_set, 1)
                pool.wait_ge(tab_loaded, 32)
                for t in range(T):
                    pool.indirect_dma_start(x1[:, t, :], None, x[:, :],
                                            bass.IndirectOffsetOnAxis(own[:, t, :], 0)).then_inc(x_got, 16)

            @block.sync
            def _(sp):
                sp.wait_ge(rec_stored, T * 16)
                ranked = record_dram.rearrange("(t p) c -> p t c", p=P)
                sp.dma_start(tab[:, 0:T - FIRST_TILE, :], ranked[:, FIRST_TILE:T, :]).then_inc(tab_loaded, 16)
                sp.dma_start(tab[:, T - FIRST_TILE:T, :], ranked[:, 0:FIRST_TILE, :]).then_inc(tab_loaded, 16)
                sp.wait_ge(s1_copied, 1)
                sp.dma_start(s1t_dram, s1t[:, :]).then_inc(s1_stored, 16)
                sp.wait_ge(s1_stored, 16)
                sp.dma_start(s1_bc[:, :, :].rearrange("p h n -> p (h n)"),
                             s1t_dram.rearrange("h n -> (h n)").partition_broadcast(P)).then_inc(s1_loaded, 16)
                sp.wait_ge(s1_loaded, 16)

            @block.tensor
            def _(pe):
                pe.wait_ge(tab_loaded, 32)
                for k in range(LONE):
                    last = pe.transpose(bank[0][0:H, k * P:(k + 1) * P], s1_rank[:, LONE0 + k, :], ident[:, :])
                last.then_inc(s1_tr, 1)

            @block.vector
            def _(dve):
                step = chain(dve, prep_step)
                dve.wait_ge(tab_loaded, 32)
                step(dve.tensor_tensor(a_fac[:, :, :], s1_rank[:, LONE0:LONE0 + LONE, :],
                                       s2_max[:, :].unsqueeze(1).to_broadcast([P, LONE, H]), ALU.add))
                step(dve.tensor_scalar(c_fac[:, :, :], a_fac[:, :, :], ALPHA - 1.0, 0.0, ALU.mult, ALU.min))
                dve.tensor_scalar(a_fac[:, :, :], a_fac[:, :, :], 1.0 - ALPHA, 0.0, ALU.mult, ALU.min).then_inc(fac_ready, 1)
                dve.wait_ge(s1_tr, 1)
                dve.tensor_copy(s1t[:, :], bank[0][0:H, 0:LN]).then_inc(s1_copied, 1)
                step(dve.tensor_tensor(valid[:, :, :], degree.unsqueeze(2).to_broadcast([P, T, TOP]),
                                       slot_no[:, :].unsqueeze(1).to_broadcast([P, T, TOP]), ALU.is_gt))
                dve.tensor_scalar(pen[:, :, :], valid[:, :, :], 1.0, FAR, ALU.subtract, ALU.mult)
                step(dve.tensor_scalar(has[:, :], degree, 1.0, None, ALU.min))
                dve.tensor_scalar(has_not[:, :], has[:, :], -1.0, 1.0, ALU.mult, ALU.add)
                dve.tensor_scalar(others[:, :], degree, -1.0, float(N), ALU.mult, ALU.add)

            @block.scalar
            def _(act):
                act.wait_ge(fac_ready, 1)
                act.activation(a_fac[:, :, :], a_fac[:, :, :], ACT.Exp)
                act.activation(c_fac[:, :, :], c_fac[:, :, :], ACT.Exp)

        wst_ready, p1_done, r1_done, p2_done, parts_free, sign_done, twos_done, mm_free, evac_free, act_own, e_step = (
            sem(k) for k in "wst_ready p1_done r1_done p2_done parts_free sign_done twos_done mm_free evac_free act_own e_step".split())
        block = nc.Block()
        with block:
            @block.vector
            def _(dve):
                cnt = [0]
                PER = 12

                def weights(g, i):
                    n = g * 2 + i
                    h = n
                    dve.wait_ge(parts_free, n + 1)
                    seq_h = seq_all[:, :, bass.ds(h * DH, DH)]
                    dve.tensor_tensor(wst[i][:, :, 0:DH], seq_h,
                                      b_exp[:, :, bass.ds(h, 1)].to_broadcast([P, T, DH]), ALU.mult)
                    dve.tensor_tensor(wst[i][:, :, DH + 1:W2 - 1], seq_h,
                                      d_exp[:, :, bass.ds(h, 1)].to_broadcast([P, T, DH]), ALU.mult)
                    dve.tensor_copy(wst[i][:, :, DH:DH + 1], b_exp[:, :, bass.ds(h, 1)])
                    dve.tensor_copy(wst[i][:, :, W2 - 1:W2], d_exp[:, :, bass.ds(h, 1)]).then_inc(wst_ready, 1)

                def twos(g):
                    n = g * 2 + 1
                    cnt[0] += 1
                    dve.wait_ge(mm_free, n + 1)
                    dve.tensor_copy(s2_col[1][:, :].unsqueeze(2), neg_s2[:, :, bass.ds(n, 1)]).then_inc(e_step, 1)
                    dve.wait_ge(e_step, g * PER + cnt[0])
                    for j in range(T):
                        last = dve.tensor_scalar(ind[1][:, j, :], s1_bc[:, bass.ds(n, 1), :].rearrange("p a n -> p (a n)"),
                                                 s2_col[1][:, j:j + 1], 2.0, ALU.is_gt, ALU.mult)
                    last.then_inc(twos_done, 1)

                def evacuate(g, i, at):
                    n = g * 2 + i

                    def step(ins):
                        cnt[0] += 1
                        ins.then_inc(e_step, 1)
                        dve.wait_ge(e_step, at * PER + cnt[0])

                    dve.wait_ge(mm_free, n + 3)
                    step(dve.tensor_reduce(ev[:, :, :], psum[:, 4 * i:4 * i + 4, 0:3 * W2].rearrange("p b (k w) -> p b w k", k=3),
                                           AX_X, ALU.add))
                    if i == 0:
                        step(dve.tensor_tensor(ev[:, 0:LONE, :], ev[:, 0:LONE, :],
                                               ev[:, LONE:LONE + 1, :].to_broadcast([P, LONE, W2]), ALU.add))
                    step(dve.scalar_tensor_tensor(dt_[:, :, :], ev[:, LONE:LONE + 1, DH + 1:W2].to_broadcast([P, LONE, DH + 1]),
                                                  2.0, ev[:, 0:LONE, DH + 1:W2], ALU.mult, ALU.subtract))
                    dve.tensor_tensor(bt[:, :, :], ev[:, 0:LONE, 0:DH + 1],
                                      a_fac[:, :, bass.ds(n, 1)].to_broadcast([P, LONE, DH + 1]), ALU.mult)
                    step(dve.tensor_tensor(dt_[:, :, :], dt_[:, :, :],
                                           c_fac[:, :, bass.ds(n, 1)].to_broadcast([P, LONE, DH + 1]), ALU.mult))
                    step(dve.tensor_tensor(bt[:, :, :], bt[:, :, :], dt_[:, :, :], ALU.add))
                    step(dve.reciprocal(rec[:, :, :], bt[:, :, DH:DH + 1]))
                    dve.tensor_tensor(lone[:, :, bass.ds(n * DH, DH)], bt[:, :, 0:DH],
                                      rec[:, :, :].to_broadcast([P, LONE, DH]), ALU.mult).then_inc(evac_free, 1)

                dve.sem_inc(evac_free, 2)
                weights(0, 0)
                weights(0, 1)
                twos(0)
                cnt[0] = 0
                with dve.Fori(1, H // 2) as g:
                    weights(g, 0)
                    weights(g, 1)
                    at = g - 1
                    cnt[0] = 1
                    evacuate(at, 0, at)
                    cnt[0] = 7
                    n = g * 2 + 1
                    dve.wait_ge(mm_free, n + 1)
                    dve.tensor_copy(s2_col[1][:, :].unsqueeze(2), neg_s2[:, :, bass.ds(n, 1)]).then_inc(e_step, 1)
                    dve.wait_ge(e_step, at * PER + 8)
                    for j in range(T):
                        last = dve.tensor_scalar(ind[1][:, j, :], s1_bc[:, bass.ds(n, 1), :].rearrange("p a n -> p (a n)"),
                                                 s2_col[1][:, j:j + 1], 2.0, ALU.is_gt, ALU.mult)
                    last.then_inc(twos_done, 1)
                    cnt[0] = 8
                    evacuate(at, 1, at)
                    assert cnt[0] == PER + 1
                cnt[0] = 1
                evacuate(H // 2 - 1, 0, H // 2 - 1)
                evacuate(H // 2 - 1, 1, H // 2 - 1)

            @block.scalar
            def _(act):
                with act.Fori(0, H // 2) as g:
                    for i in range(2):
                        n = g * 2 + i
                        act.wait_ge(wst_ready, n + 1)
                        act.wait_ge(mm_free, n + 1)
                        act.activation(parts[i][:, :, 0, :], wst[i][:, :, :], ACT.Copy).then_inc(p1_done, 1)
                    act.activation(s2_col[0][:, :].unsqueeze(2), seq_all[:, :, bass.ds(g * 2 + D, 1)], ACT.Copy).then_inc(act_own, 1)
                    act.wait_ge(act_own, g + 1)
                    for j in range(T):
                        if j == T // 2:
                            for i in range(2):
                                act.wait_ge(r1_done, g * 2 + i + 1)
                                act.activation(parts[i][:, :, 1, :], wst[i][:, :, :], ACT.Copy).then_inc(p2_done, 1)
                        last = act.activation(ind[0][:, j, :], s1_bc[:, bass.ds(g * 2, 1), :].rearrange("p a n -> p (a n)"),
                                              ACT.Sign, bias=s2_col[0][:, j:j + 1])
                    last.then_inc(sign_done, 1)

            @block.gpsimd
            def _(pool):
                pool.sem_inc(parts_free, 2)
                with pool.Fori(0, H // 2) as g:
                    for i in range(2):
                        pool.wait_ge(p1_done, g * 2 + i + 1)
                        pool.tensor_tensor(wst[i][:, :, :], wst[i][:, :, :], parts[i][:, :, 0, :], ALU.subtract).then_inc(r1_done, 1)
                    for i in range(2):
                        pool.wait_ge(p2_done, g * 2 + i + 1)
                        pool.tensor_tensor(parts[i][:, :, 2, :], wst[i][:, :, :], parts[i][:, :, 1, :], ALU.subtract).then_inc(parts_free, 1)

            @block.tensor
            def _(pe):
                pe.sem_inc(mm_free, 2)
                with pe.Fori(0, H // 2) as g:
                    for i in range(2):
                        n = g * 2 + i
                        pe.wait_ge(parts_free, n + 3)
                        pe.wait_ge((sign_done, twos_done)[i], g + 1)
                        pe.wait_ge(evac_free, n + 1)
                        for j in range(T):
                            rhs = parts[i][:, j, :, :].rearrange("p k w -> p (k w)")
                            for k in range(LONE):
                                pe.matmul(bank[4 * i + k][:, 0:3 * W2], ind[i][:, j, k * P:(k + 1) * P], rhs,
                                          start=(j == 0), stop=(j == T - 1))
                            last = pe.matmul(bank[4 * i + LONE][:, 0:3 * W2], ones_b[:, :], rhs,
                                             start=(j == 0), stop=(j == T - 1))
                        last.then_inc(mm_free, 1)
        lone_ctx.close()

        got0 = [sem(f"got0_{t}") for t in range(T)]
        got1 = [sem(f"got1_{t}") for t in range(T)]
        sc_ready, sc_exp, hid_ready, hid_tr, hidT_done, proj_done, elu_in, elu_exp, var_ready, rstd_ready, ln_ready, h1_done = (
            sem(k) for k in "sc_ready sc_exp hid_ready hid_tr hidT_done proj_done elu_in elu_exp var_ready rstd_ready ln_ready h1_done".split())
        h1_tr, h1T_done, u_done, u_copied, g_step = (sem(k) for k in "h1_tr h1T_done u_done u_copied g_step".split())
        h1_stored = [sem(f"h1_stored{i}") for i in range(2)]
        u_all = seq_all
        l0 = ctx.enter_context(ExitStack())
        G = sb("G", [P, REUSE, SG], stack=l0)
        sc = sb("sc", [P, NSLOT, H], stack=l0)
        top = sb("top", [P, T, H], stack=l0)
        hid = v["w_seq"][:, 0:2, :]
        tmp = v["w_seq"][:, 2:4, :]
        y = sb("y", [P, 2, D], stack=l0)
        e = sb("e", [P, 2, D], stack=l0)
        st6, mv2, ve, rs, nm = (sb(k, [P, 2, w], stack=l0) for k, w in (("st6", 6), ("mv2", 2), ("ve", 1), ("rs", 1), ("nm", 1)))
        hidT = hT[:, 0, :]
        h1T = hT[:, 1, :]

        h_acc = sb("h_acc", [P, D], stack=l0)
        summed = sem("summed")

        def run_of(t):
            for r in RUNS:
                if r[0] == t:
                    return r
            return None

        block = nc.Block()
        with block:
            @block.gpsimd
            def _(pool):
                def gather(t):
                    if FIRST_SLOT[t] >= REUSE:
                        last_slot = FIRST_SLOT[t + 1] - 1 - REUSE
                        pool.wait_ge(hid_ready, sum(f <= last_slot for f in FIRST_SLOT[:T]))
                    for s in range(SLOTS[t]):
                        pool.indirect_dma_start(G[:, (FIRST_SLOT[t] + s) % REUSE, :], None, seq_dram[:, :],
                                                bass.IndirectOffsetOnAxis(tab[:, t, s:s + 1], 0)).then_inc(got0[t], 16)
                for t in range(GATHERED):
                    gather(t)
                for t in range(T):
                    pool.wait_ge(var_ready, t + 1)
                    pool.tensor_tensor(rs[:, t % 2, :], ve[:, t % 2, :], power[:, :], ALU.pow).then_inc(rstd_ready, 1)
                    pool.wait_ge(h1_done, t + 1)
                    pool.indirect_dma_start(h1_dram[:, :], bass.IndirectOffsetOnAxis(own[:, t, :], 0),
                                            h_t[:, t % 2, :], None).then_inc(h1_stored[t % 2], 16)
                    if t:
                        pool.wait_ge(summed, t)
                        pool.tensor_tensor(h_acc[:, :], h_acc[:, :], h_t[:, t % 2, :], ALU.add).then_inc(summed, 1)
                    else:
                        pool.tensor_copy(h_acc[:, :], h_t[:, 0, :]).then_inc(summed, 1)
                    r = run_of(t + AHEAD)
                    if r and r[0] >= GATHERED:
                        for k in range(r[0], r[0] + r[1]):
                            gather(k)
                for i in range(2):
                    pool.wait_ge(h1_stored[i], T // 2 * 16)

            @block.vector
            def _(dve):
                step = chain(dve, g_step)
                runs_done, last_x1 = [0], [None]

                def scores(r):
                    t0, n, K = r
                    o = FIRST_SLOT[t0]
                    seg = sc[:, o:o + n * K, :].rearrange("p (n k) h -> p n k h", k=K)
                    for t in range(t0, t0 + n):
                        dve.wait_ge(got0[t], 16 * K)
                    s1 = s1_rank[:, t0:t0 + n, :].unsqueeze(2).to_broadcast([P, n, K, H])
                    step(dve.tensor_tensor(seg, G[:, o % REUSE:o % REUSE + n * K, D:SG].rearrange("p (n k) h -> p n k h", k=K), s1, ALU.add))
                    step(dve.scalar_tensor_tensor(seg, seg, ALPHA, seg, ALU.mult, ALU.max))
                    step(dve.tensor_tensor(seg, seg, pen[:, t0:t0 + n, 0:K].unsqueeze(3).to_broadcast([P, n, K, H]), ALU.add))
                    step(dve.tensor_reduce(top[:, t0:t0 + n, :], seg.rearrange("p n k h -> p n h k"), AX_X, ALU.max))
                    dve.tensor_tensor(seg, seg, top[:, t0:t0 + n, :].unsqueeze(2).to_broadcast([P, n, K, H]),
                                      ALU.subtract).then_inc(sc_ready, 1)

                def normalise(r):
                    t0, n, K = r
                    o = FIRST_SLOT[t0]
                    seg = sc[:, o:o + n * K, :].rearrange("p (n k) h -> p n k h", k=K)
                    runs_done[0] += 1
                    dve.wait_ge(sc_exp, runs_done[0])
                    step(dve.tensor_reduce(top[:, t0:t0 + n, :], seg.rearrange("p n k h -> p n h k"), AX_X, ALU.add))
                    step(dve.reciprocal(top[:, t0:t0 + n, :], top[:, t0:t0 + n, :]))
                    step(dve.tensor_tensor(seg, seg, top[:, t0:t0 + n, :].unsqueeze(2).to_broadcast([P, n, K, H]), ALU.mult))

                def weighted(o, dst):
                    return dve.tensor_tensor(dst.rearrange("p (h d) -> p h d", h=H),
                                             G[:, o % REUSE, 0:D].rearrange("p (h d) -> p h d", h=H),
                                             sc[:, o, :].unsqueeze(2).to_broadcast([P, H, DH]), ALU.mult)

                def aggregate(t):
                    hb = hid[:, t % 2, :]
                    if t >= 2:
                        dve.wait_ge(hid_tr, t - 1)
                    if not SLOTS[t]:
                        dve.tensor_copy(hb, lone[:, t - LONE0, :]).then_inc(hid_ready, 1)
                        return
                    last = weighted(FIRST_SLOT[t], hb)
                    for s in range(1, SLOTS[t]):
                        tb = tmp[:, s % 2, :]
                        step(last)
                        step(weighted(FIRST_SLOT[t] + s, tb))
                        last = dve.tensor_tensor(hb, hb, tb, ALU.add)
                    if LONE0 <= t < LONE0 + LONE:
                        step(last)
                        step(dve.tensor_scalar(hb, hb, has[:, t:t + 1], None, ALU.mult))
                        last = dve.scalar_tensor_tensor(hb, lone[:, t - LONE0, :], has_not[:, t:t + 1], hb, ALU.mult, ALU.add)
                    last.then_inc(hid_ready, 1)

                def elu_a(t):
                    b = t % 2
                    dve.wait_ge(proj_done, t + 1)
                    step(dve.tensor_tensor(y[:, b, :], bank[2 + b], bout_bc[:, :], ALU.add))
                    dve.tensor_scalar(e[:, b, :], y[:, b, :], 0.0, None, ALU.min).then_inc(elu_in, 1)
                    last_x1[0] = dve.scalar_tensor_tensor(x1[:, t, :], y[:, b, :], 0.0, x1[:, t, :], ALU.max, ALU.add)

                def elu_b(t):
                    b = t % 2
                    dve.wait_ge(elu_exp, t + 1)
                    step(dve.scalar_tensor_tensor(x1[:, t, :], e[:, b, :], -1.0, x1[:, t, :], ALU.add, ALU.add))
                    step(dve.bn_stats(st6[:, b, :], x1[:, t, :]))
                    step(dve.bn_aggr(mv2[:, b, :], st6[:, b, :]))
                    dve.tensor_scalar(ve[:, b, :], mv2[:, b, 1:2], EPS, None, ALU.add).then_inc(var_ready, 1)

                def norm_bias(t):
                    b = t % 2
                    dve.wait_ge(rstd_ready, t + 1)
                    dve.scalar_tensor_tensor(nm[:, b, :], mv2[:, b, 0:1], -1.0, rs[:, b, :], ALU.mult, ALU.mult).then_inc(ln_ready, 1)

                def copy_u(t):
                    dve.wait_ge(u_done, t + 1)
                    dve.tensor_tensor(u_all[:, t, 0:D], bank[4 + t % 2], u_bias_bc[:, :], ALU.add).then_inc(u_copied, 1)

                dve.wait_ge(x_got, T * 16)
                for k in range(T + 5):
                    r = run_of(k)
                    if r:
                        scores(r)
                    if 3 <= k < T + 3:
                        norm_bias(k - 3)
                    if r:
                        normalise(r)
                    if k < T:
                        aggregate(k)
                    if 2 <= k < T + 2:
                        elu_a(k - 2)
                    if k >= 5:
                        step(last_x1[0]) if k < T + 2 else None
                        copy_u(k - 5)
                    elif k >= 2:
                        step(last_x1[0])
                    if 2 <= k < T + 2:
                        elu_b(k - 2)

            @block.scalar
            def _(act):
                runs = [0]
                for k in range(T + 3):
                    r = run_of(k)
                    if r:
                        t0, n, K = r
                        o = FIRST_SLOT[t0]
                        runs[0] += 1
                        act.wait_ge(sc_ready, runs[0])
                        act.activation(sc[:, o:o + n * K, :], sc[:, o:o + n * K, :], ACT.Exp).then_inc(sc_exp, 1)
                    if k >= 3:
                        t = k - 3
                        act.wait_ge(ln_ready, t + 1)
                        if t >= 2:
                            act.wait_ge(h1_tr, t - 1)
                            act.wait_ge(summed, t - 1)
                            act.wait_ge(h1_stored[t % 2], 16 * (t // 2))
                        act.activation(h_t[:, t % 2, :], x1[:, t, :], ACT.Relu, bias=nm[:, t % 2, :],
                                       scale=rs[:, t % 2, :]).then_inc(h1_done, 1)
                    if k < T:
                        act.wait_ge(hid_tr, k + 1)
                        if k:
                            act.wait_ge(proj_done, k)
                        act.activation(hidT, bank[0], ACT.Copy).then_inc(hidT_done, 1)
                    if 2 <= k < T + 2:
                        act.wait_ge(elu_in, k - 1)
                        act.activation(e[:, k % 2, :], e[:, k % 2, :], ACT.Exp).then_inc(elu_exp, 1)
                    if k >= 3:
                        act.wait_ge(h1_tr, k - 2)
                        if k >= 4:
                            act.wait_ge(u_done, k - 3)
                        act.activation(h1T, bank[1], ACT.Copy).then_inc(h1T_done, 1)

            @block.tensor
            def _(pe):
                for k in range(T + 4):
                    if k < T:
                        pe.wait_ge(hid_ready, k + 1)
                        if k:
                            pe.wait_ge(hidT_done, k)
                        for c in range(C):
                            last = pe.transpose(bank[0][:, c * P:(c + 1) * P], hid[:, k % 2, c * P:(c + 1) * P], ident[:, :])
                        last.then_inc(hid_tr, 1)
                    if k >= 4:
                        t = k - 4
                        pe.wait_ge(h1T_done, t + 1)
                        if t >= 2:
                            pe.wait_ge(u_copied, t - 1)
                        for c in range(C):
                            pe.matmul(bank[4 + t % 2], h1T[:, c * P:(c + 1) * P], w_qk[:, c, :],
                                      start=(c == 0), stop=(c == C - 1))
                        for c in range(C):
                            last = pe.matmul(bank[6][:, t:t + 1], h1T[:, c * P:(c + 1) * P], c_vec[:, c:c + 1],
                                             start=(c == 0), stop=(c == C - 1))
                        last.then_inc(u_done, 1)
                    if 3 <= k < T + 3:
                        t = k - 3
                        pe.wait_ge(h1_done, t + 1)
                        if t:
                            pe.wait_ge(h1T_done, t)
                        for c in range(C):
                            last = pe.transpose(bank[1][:, c * P:(c + 1) * P], h_t[:, t % 2, c * P:(c + 1) * P], ident[:, :])
                        last.then_inc(h1_tr, 1)
                    if k < T:
                        pe.wait_ge(hidT_done, k + 1)
                        if k >= 2:
                            pe.wait_ge(elu_in, k - 1)
                        for c in range(C):
                            last = pe.matmul(bank[2 + k % 2], hidT[:, c * P:(c + 1) * P], w_out[:, c, :],
                                             start=(c == 0), stop=(c == C - 1))
                        last.then_inc(proj_done, 1)
                pe.wait_ge(summed, T)
                pe.matmul(bank[7], ones[:, 0:P], h_acc[:, :])
        l0.close()

        z_ready, z_exp, agg_ready, a_tr, aT_done, o_done, o_ready, z_step, dot_done, base_ready, sums_ready, weights_ready = (
            sem(k) for k in "z_ready z_exp agg_ready a_tr aT_done o_done o_ready z_step dot_done base_ready sums_ready weights_ready".split())
        out_stored = [sem(f"out_stored{i}") for i in range(2)]
        l1 = ctx.enter_context(ExitStack())
        G1 = sb("G1", [P, REUSE, D], stack=l1)
        z = sb("z", [P, NSLOT], stack=l1)
        zq = sb("zq", [P, NSLOT], stack=l1)
        zc = sb("zc", [P, T], stack=l1)
        zm, e0, den, z_t = (sb(k, [P, T], stack=l1) for k in ("zm", "e0", "den", "z_t"))
        h_sum = sb("h_sum", [P, D], stack=l1)
        junk = sb("junk", [P, 2, D], stack=l1)
        y1 = sb("y1", [P, 2, D], stack=l1)
        o_t = sb("o_t", [P, 2, D], stack=l1)
        NONE = -10000.0
        with_slots = [sum(n > 0 for n in SLOTS[:k]) for k in range(T + 1)]
        block = nc.Block()
        with block:
            @block.gpsimd
            def _(pool):
                def gather(t):
                    if FIRST_SLOT[t] >= REUSE:
                        last_slot = FIRST_SLOT[t + 1] - 1 - REUSE
                        pool.wait_ge(agg_ready, with_slots[sum(f <= last_slot for f in FIRST_SLOT[:T])])
                    for s in range(SLOTS[t]):
                        pool.indirect_dma_start(G1[:, (FIRST_SLOT[t] + s) % REUSE, :], None, h1_dram[:, :],
                                                bass.IndirectOffsetOnAxis(tab[:, t, s:s + 1], 0)).then_inc(got1[t], 16)
                for t in range(GATHERED):
                    gather(t)
                for t in range(T):
                    pool.wait_ge(o_ready, t + 1)
                    pool.indirect_dma_start(out[:, :], bass.IndirectOffsetOnAxis(own[:, t, :], 0),
                                            o_t[:, t % 2, :], None).then_inc(out_stored[t % 2], 16)
                    r = run_of(t + AHEAD)
                    if r and r[0] >= GATHERED:
                        for k in range(r[0], r[0] + r[1]):
                            gather(k)
                for i in range(2):
                    pool.wait_ge(out_stored[i], T // 2 * 16)

            @block.vector
            def _(dve):
                step = chain(dve, z_step)
                runs_done, dots = [0], [0]

                def views(r):
                    t0, n, K = r
                    o = FIRST_SLOT[t0]
                    return t0, n, K, *(a[:, o:o + n * K].rearrange("p (n k) -> p n k", k=K) for a in (z, zq))

                def bc(a, t0, n, K):
                    return a[:, t0:t0 + n].unsqueeze(2).to_broadcast([P, n, K])

                def scores(r):
                    t0, n, K, zz, qq = views(r)
                    for t in range(t0, t0 + n):
                        dve.wait_ge(got1[t], 16 * K)
                        for s in range(K):
                            k = FIRST_SLOT[t] + s
                            dots[0] += 1
                            if dots[0] > 2:
                                dve.wait_ge(dot_done, dots[0] - 2)
                            dve.tensor_tensor_reduce(junk[:, k % 2, :], u_all[:, t, 0:D], G1[:, k % REUSE, :], 1.0, 0.0,
                                                     ALU.mult, ALU.add, z[:, k:k + 1]).then_inc(dot_done, 1)
                    dve.wait_ge(dot_done, dots[0])
                    step(dve.tensor_tensor(zz, zz, bc(zc, t0, n, K), ALU.add))
                    step(dve.tensor_scalar(zz, zz, SCALE, None, ALU.mult))
                    step(dve.tensor_scalar(qq, zz, 0.0, NONE, ALU.is_equal, ALU.mult))
                    step(dve.tensor_tensor(zz, zz, qq, ALU.add))
                    step(dve.tensor_tensor(zz, zz, pen[:, t0:t0 + n, 0:K], ALU.add))
                    m = zm[:, t0:t0 + n]
                    step(dve.tensor_reduce(m, zz, AX_X, ALU.max))
                    step(dve.tensor_scalar(m, m, NONE, None, ALU.max))
                    dve.tensor_scalar(e0[:, t0:t0 + n], m, NONE, -1.0, ALU.subtract, ALU.mult)
                    dve.tensor_tensor(zz, zz, bc(zm, t0, n, K), ALU.subtract).then_inc(z_ready, 1)

                def normalise(r):
                    t0, n, K, zz, qq = views(r)
                    d, e_, t_ = (a[:, t0:t0 + n] for a in (den, e0, z_t))
                    runs_done[0] += 1
                    dve.wait_ge(z_exp, runs_done[0])
                    step(dve.tensor_reduce(d, zz, AX_X, ALU.add))
                    step(dve.tensor_tensor(t_, e_, others[:, t0:t0 + n], ALU.mult))
                    step(dve.tensor_tensor(d, d, t_, ALU.add))
                    step(dve.reciprocal(d, d))
                    step(dve.tensor_tensor(qq, valid[:, t0:t0 + n, 0:K], bc(e0, t0, n, K), ALU.mult))
                    step(dve.tensor_tensor(zz, zz, qq, ALU.subtract))
                    dve.tensor_tensor(zz, zz, bc(den, t0, n, K), ALU.mult)
                    dve.tensor_tensor(e_, e_, d, ALU.mult).then_inc(weights_ready, 1)
                    dve.wait_ge(weights_ready, runs_done[0])

                def aggregate(t):
                    hb = h_t[:, t % 2, :]
                    dve.wait_ge(base_ready, t + 1)
                    for s in range(SLOTS[t]):
                        k = FIRST_SLOT[t] + s
                        last = dve.scalar_tensor_tensor(hb, G1[:, k % REUSE, :], z[:, k:k + 1], hb, ALU.mult, ALU.add)
                        if s < SLOTS[t] - 1:
                            step(last)
                        else:
                            last.then_inc(agg_ready, 1)

                def finish(t):
                    dve.wait_ge(o_done, t + 1)
                    step(dve.tensor_tensor(y1[:, t % 2, :], bank[2 + t % 4], bv_bc[:, :], ALU.add))
                    if t >= 2:
                        dve.wait_ge(out_stored[t % 2], 16 * (t // 2))
                    dve.scalar_tensor_tensor(o_t[:, t % 2, :], y1[:, t % 2, :], 0.0, x1[:, t, :], ALU.max, ALU.add).then_inc(o_ready, 1)

                dve.tensor_copy(h_sum[:, :], bank[7]).then_inc(sums_ready, 1)
                step(dve.tensor_scalar(zc[:, :], bank[6][:, 0:T], bqk[:, :], None, ALU.add))
                for k in range(T + 2):
                    r = run_of(k)
                    if r:
                        scores(r)
                        if k >= 2:
                            finish(k - 2)
                        normalise(r)
                    if k < T and SLOTS[k]:
                        aggregate(k)
                    if k >= 2 and not r:
                        finish(k - 2)

            @block.scalar
            def _(act):
                runs = [0]

                def base_of(t):
                    if t >= 2:
                        act.wait_ge(a_tr, t - 1)
                    if run_of(t):
                        act.wait_ge(weights_ready, runs[0])
                    if SLOTS[t]:
                        act.activation(h_t[:, t % 2, :], h_sum[:, :], ACT.Copy, scale=e0[:, t:t + 1]).then_inc(base_ready, 1)
                    else:
                        act.activation(h_t[:, t % 2, :], h_sum[:, :], ACT.Copy, scale=1.0 / N).then_inc(base_ready, 1)

                act.wait_ge(sums_ready, 1)
                for k in range(T):
                    r = run_of(k)
                    if r:
                        t0, n, K = r
                        o = FIRST_SLOT[t0]
                        runs[0] += 1
                        act.wait_ge(z_ready, runs[0])
                        act.activation(z[:, o:o + n * K], z[:, o:o + n * K], ACT.Exp)
                        act.activation(e0[:, t0:t0 + n], e0[:, t0:t0 + n], ACT.Exp).then_inc(z_exp, 1)
                        base_of(k)
                    if k + 1 < T and not run_of(k + 1):
                        base_of(k + 1)
                    act.wait_ge(a_tr, k + 1)
                    if k >= 2:
                        act.wait_ge(o_done, k - 1)
                    act.activation(hT[:, k % 2, :], bank[k % 2], ACT.Copy).then_inc(aT_done, 1)

            @block.tensor
            def _(pe):
                for k in range(T + 1):
                    if k < T:
                        if SLOTS[k]:
                            pe.wait_ge(agg_ready, with_slots[k + 1])
                        else:
                            pe.wait_ge(base_ready, k + 1)
                        if k >= 2:
                            pe.wait_ge(aT_done, k - 1)
                        for c in range(C):
                            last = pe.transpose(bank[k % 2][:, c * P:(c + 1) * P], h_t[:, k % 2, c * P:(c + 1) * P], ident[:, :])
                        last.then_inc(a_tr, 1)
                    if k >= 1:
                        t = k - 1
                        pe.wait_ge(aT_done, t + 1)
                        if t >= 4:
                            pe.wait_ge(o_ready, t - 3)
                        for c in range(C):
                            last = pe.matmul(bank[2 + t % 4], hT[:, t % 2, c * P:(c + 1) * P], wv_t[:, c, :],
                                             start=(c == 0), stop=(c == C - 1))
                        last.then_inc(o_done, 1)


def dense_layers(nc, v):
    ctx = ExitStack()
    (x, adj, out, bank, ident, ones, seq_all, w_out, w_qk, wv_t, bout_bc, bv_bc, u_bias, c_vec, bqk, s2t_dram,
     h_t, hT) = (v[k] for k in (
        "x adj out bank ident ones seq_all w_out w_qk wv_t bout_bc bv_bc u_bias c_vec bqk s2t_dram h_t hT").split())
    with ctx:
        def sb(name, shape, dt=F32):
            return ctx.enter_context(nc.sbuf_tensor(name, shape, dt))

        def sem(name):
            return ctx.enter_context(nc.semaphore("dense_" + name))

        h1 = sb("d_h1", [P, T, D])
        h1T = sb("d_h1T", [P, C, N])
        adj_t = sb("d_adj", [P, N])
        s2_bc = sb("d_s2", [P, N])
        z = sb("d_z", [P, N])
        s2t = s2_bc
        eT = sb("d_eT", [P, N])
        eT2 = eT
        hid, xt, y, e = sb("d_hid", [P, D]), sb("d_x", [P, D]), sb("d_y", [P, D]), sb("d_e", [P, D])
        uT = sb("d_uT", [P, C, P])
        cT = sb("d_cT", [1, P])
        small = sb("d_small", [P, 8])
        st6 = sb("d_st6", [P, 6])
        mv2 = sb("d_mv2", [P, 2])
        x1_dram = nc.dram_tensor("x1_dram", [N, D], F32, kind="Internal").ap()

        s2_tr, s2_copied, s2_stored = sem("s2_tr"), sem("s2_copied"), sem("s2_stored")
        adj_loaded, x_loaded, s2_loaded = sem("adj_loaded"), sem("x_loaded"), sem("s2_loaded")
        pen_ready, score_ready, exp_done, tr_done, eT_done, pv_done, head_done = (
            sem(s) for s in "pen_ready score_ready exp_done tr_done eT_done pv_done head_done".split())
        hidT_tr, hidT_done, proj_done, y_ready, elu_exp, ln_ready, h1_done, h1_tr, h1T_done, x1_stored, x1_ready = (
            sem(s) for s in "hidT_tr hidT_done proj_done y_ready elu_exp ln_ready h1_done h1_tr h1T_done x1_stored x1_ready".split())
        dve_step = sem("dve_step")
        var_ready, rstd_ready = sem("var_ready"), sem("rstd_ready")
        tail_step, l1_step, out_stored = sem("tail_step"), sem("l1_step"), sem("out_stored")
        adj2_loaded, x2_loaded = sem("adj2_loaded"), sem("x2_loaded")
        u_done, u_copied, z_done, z_ready, p_done, p_tr, pT_done, agg_done, agg_ready, aT_tr, aT_done, o_done, o_ready = (
            sem(s) for s in "u_done u_copied z_done z_ready p_done p_tr pT_done agg_done agg_ready aT_tr aT_done o_done o_ready".split())

        def col(ap, t, lo, hi):
            return ap[:, bass.ds(t, 1), lo:hi].rearrange("p a n -> p (a n)")

        block = nc.Block()
        with block:
            @block.tensor
            def _(pe):
                for t in range(T):
                    last = pe.transpose(bank[t // 4][0:H, (t % 4) * P:(t % 4 + 1) * P], seq_all[:, t, D:D + H], ident[:, :])
                last.then_inc(s2_tr, 1)

            @block.vector
            def _(dve):
                dve.wait_ge(s2_tr, 1)
                for k in range(4):
                    last = dve.tensor_copy(s2t[0:H, k * 512:(k + 1) * 512], bank[k][0:H, :])
                    last.then_inc(s2_copied, 1)

            @block.sync
            def _(sp):
                sp.wait_ge(s2_copied, 4)
                sp.dma_start(s2t_dram, s2t[0:H, :]).then_inc(s2_stored, 16)
                sp.wait_ge(s2_stored, 16)

        block = nc.Block()
        with block:
            @block.gpsimd
            def _(pool):
                with pool.Fori(0, T) as t:
                    pool.wait_ge(var_ready, t + 1)
                    pool.tensor_tensor(small[:, 3:4], small[:, 5:6], v["power"][:, :], ALU.pow).then_inc(rstd_ready, 1)

            @block.sync
            def _(sp):
                with sp.Fori(0, T) as t:
                    sp.dma_start(adj_t[:, :], adj[bass.ds(t * P, P), :]).then_inc(adj_loaded, 16)
                    sp.dma_start(xt[:, :], x[bass.ds(t * P, P), :]).then_inc(x_loaded, 16)
                    with sp.Fori(0, H) as h:
                        k = t * H + h
                        sp.wait_ge(pv_done, k + 1)
                        sp.dma_start(s2_bc[:, :], s2t_dram[bass.ds(h, 1), :].rearrange("a n -> (a n)").partition_broadcast(P)).then_inc(s2_loaded, 16)
                    sp.wait_ge(h1_done, t + 1)
                    sp.dma_start(x1_dram[bass.ds(t * P, P), :], y[:, :]).then_inc(x1_stored, 16)
                    sp.wait_ge(x1_stored, t * 16 + 16)
                    sp.sem_inc(x1_ready, 1)
                sp.wait_ge(x1_stored, T * 16)

            def dve_tail(dve, t):
                at = t * 6
                dve.wait_ge(proj_done, t + 1)
                dve.wait_ge(x_loaded, t * 16 + 16)
                dve.tensor_tensor(y[:, :], bank[4][:, :], bout_bc[:, :], ALU.add).then_inc(tail_step, 1)
                dve.wait_ge(tail_step, at + 1)
                dve.tensor_scalar(e[:, :], y[:, :], 0.0, None, ALU.min).then_inc(y_ready, 1)
                dve.scalar_tensor_tensor(y[:, :], y[:, :], 0.0, xt[:, :], ALU.max, ALU.add).then_inc(tail_step, 1)
                dve.wait_ge(tail_step, at + 2)
                dve.wait_ge(elu_exp, t + 1)
                dve.scalar_tensor_tensor(y[:, :], e[:, :], -1.0, y[:, :], ALU.add, ALU.add).then_inc(tail_step, 1)
                dve.wait_ge(tail_step, at + 3)
                dve.bn_stats(st6[:, :], y[:, :]).then_inc(tail_step, 1)
                dve.wait_ge(tail_step, at + 4)
                dve.memset(v["gate"][:, :], 0.0)
                dve.bn_aggr(mv2[:, :], st6[:, :]).then_inc(tail_step, 1)
                dve.wait_ge(tail_step, at + 5)
                dve.tensor_scalar(small[:, 5:6], mv2[:, 1:2], EPS, None, ALU.add).then_inc(var_ready, 1)
                dve.wait_ge(rstd_ready, t + 1)
                dve.scalar_tensor_tensor(small[:, 4:5], mv2[:, 0:1], -1.0, small[:, 3:4], ALU.mult, ALU.mult).then_inc(ln_ready, 1)
                dve.wait_ge(h1_done, t + 1)
                dve.tensor_copy(col(h1, t, 0, D), h_t[:, 0, :]).then_inc(tail_step, 1)
                dve.wait_ge(tail_step, at + 6)

            @block.vector
            def _(dve):
                with dve.Fori(0, T) as t:
                    dve.wait_ge(adj_loaded, t * 16 + 16)
                    dve.tensor_scalar(adj_t[:, :], adj_t[:, :], 1.0, MASK, ALU.subtract, ALU.mult).then_inc(pen_ready, 1)
                    dve.wait_ge(pen_ready, t + 1)
                    dve.memset(v["gate"][:, :], 0.0)
                    with dve.Fori(0, H) as h:
                        k = t * H + h
                        at = k * 3
                        dve.wait_ge(s2_loaded, k * 16 + 16)
                        dve.tensor_scalar(s2_bc[:, :], s2_bc[:, :], seq_all[:, :, :].rearrange("p t n -> p (t n)")[:, bass.ds(t * SX + h + (D + H), 1)],
                                          None, ALU.add).then_inc(dve_step, 1)
                        dve.wait_ge(dve_step, at + 1)
                        dve.scalar_tensor_tensor(z[:, :], s2_bc[:, :], ALPHA, s2_bc[:, :], ALU.mult, ALU.max).then_inc(dve_step, 1)
                        dve.wait_ge(dve_step, at + 2)
                        dve.tensor_tensor(z[:, :], z[:, :], adj_t[:, :], ALU.add).then_inc(dve_step, 1)
                        dve.wait_ge(dve_step, at + 3)
                        dve.tensor_reduce(small[:, 0:1], z[:, :], AX_X, ALU.max, negate=True).then_inc(score_ready, 1)
                        for q in range(4):
                            dve.wait_ge(tr_done, k * 4 + q + 1)
                            dve.tensor_copy(eT[:, q * 512:(q + 1) * 512], bank[q % 2][:, :]).then_inc(eT_done, 1)
                        dve.wait_ge(exp_done, k + 1)
                        dve.reciprocal(small[:, 2:3], small[:, 1:2]).then_inc(head_done, 1)
                        dve.wait_ge(head_done, k * 2 + 1)
                        dve.wait_ge(pv_done, k + 2)
                        dve.tensor_scalar(hid[:, bass.ds(h * DH, DH)], bank[2][:, 0:DH], small[:, 2:3], None, ALU.mult).then_inc(head_done, 1)
                        dve.wait_ge(head_done, k * 2 + 2)
                    dve_tail(dve, t)

            @block.scalar
            def _(act):
                with act.Fori(0, T) as t:
                    with act.Fori(0, H) as h:
                        k = t * H + h
                        act.wait_ge(score_ready, k + 1)
                        act.activation(z[:, :], z[:, :], ACT.Exp, bias=small[:, 0:1], accum_out=small[:, 1:2]).then_inc(exp_done, 1)
                    act.wait_ge(hidT_tr, t + 1)
                    act.activation(hT[:, 0, :], bank[3][:, :], ACT.Copy).then_inc(hidT_done, 1)
                    act.wait_ge(y_ready, t + 1)
                    act.activation(e[:, :], e[:, :], ACT.Exp).then_inc(elu_exp, 1)
                    act.wait_ge(ln_ready, t + 1)
                    act.activation(h_t[:, 0, :], y[:, :], ACT.Relu, bias=small[:, 4:5], scale=small[:, 3:4]).then_inc(h1_done, 1)
                    act.wait_ge(h1_tr, t + 1)
                    act.activation(h1T[:, :, bass.ds(t * P, P)],
                                   bank[5][:, :].rearrange("p (c n) -> p c n", c=C), ACT.Copy).then_inc(h1T_done, 1)

            @block.tensor
            def _(pe):
                pe.transpose(bank[2][:, 0:P], ident[:, :], ident[:, :]).then_inc(pv_done, 1)
                with pe.Fori(0, T) as t:
                    with pe.Fori(0, H) as h:
                        k = t * H + h
                        pe.wait_ge(exp_done, k + 1)
                        for q in range(4):
                            if q >= 2:
                                pe.wait_ge(eT_done, k * 4 + q - 1)
                            for i in range(4):
                                j = q * 4 + i
                                last = pe.transpose(bank[q % 2][:, i * P:(i + 1) * P], z[:, j * P:(j + 1) * P], ident[:, :])
                            last.then_inc(tr_done, 1)
                        pe.wait_ge(eT_done, k * 4 + 4)
                        for j in range(T):
                            last = pe.matmul(bank[2][:, 0:DH], eT[:, j * P:(j + 1) * P],
                                             seq_all[:, j, :][:, bass.ds(h * DH, DH)], start=(j == 0), stop=(j == T - 1))
                        last.then_inc(pv_done, 1)
                    pe.wait_ge(head_done, (t + 1) * (2 * H))
                    for c in range(C):
                        last = pe.transpose(bank[3][:, c * P:(c + 1) * P], hid[:, c * P:(c + 1) * P], ident[:, :])
                    last.then_inc(hidT_tr, 1)
                    pe.wait_ge(hidT_done, t + 1)
                    for c in range(C):
                        last = pe.matmul(bank[4][:, :], hT[:, 0, c * P:(c + 1) * P], w_out[:, c, :],
                                         start=(c == 0), stop=(c == C - 1))
                    last.then_inc(proj_done, 1)
                    pe.wait_ge(h1_done, t + 1)
                    for c in range(C):
                        last = pe.transpose(bank[5][:, c * P:(c + 1) * P], h_t[:, 0, c * P:(c + 1) * P], ident[:, :])
                    last.then_inc(h1_tr, 1)
                    pe.wait_ge(h1T_done, t + 1)

        block = nc.Block()
        with block:
            @block.sync
            def _(sp):
                with sp.Fori(0, T) as t:
                    sp.wait_ge(o_ready, t + 1)
                    sp.dma_start(adj_t[:, :], adj[bass.ds(t * P, P), :]).then_inc(adj2_loaded, 16)
                    sp.dma_start(xt[:, :], x1_dram[bass.ds(t * P, P), :]).then_inc(x2_loaded, 16)
                    sp.wait_ge(o_ready, t + 2)
                    sp.dma_start(out[bass.ds(t * P, P), :], y[:, :]).then_inc(out_stored, 16)
                sp.wait_ge(out_stored, T * 16)

            @block.vector
            def _(dve):
                dve.memset(small[:, 7:8], 0.0).then_inc(o_ready, 1)
                with dve.Fori(0, T) as t:
                    at = t * 9
                    dve.wait_ge(adj2_loaded, t * 16 + 16)
                    for q in range(4):
                        dve.wait_ge(z_done, t * 4 + q + 1)
                        dve.scalar_tensor_tensor(z[:, q * 512:(q + 1) * 512], bank[q][:, :], SCALE,
                                                 adj_t[:, q * 512:(q + 1) * 512], ALU.mult, ALU.mult).then_inc(l1_step, 1)
                    dve.wait_ge(l1_step, at + 4)
                    dve.tensor_scalar(s2_bc[:, :], z[:, :], 0.0, -10000.0, ALU.is_equal, ALU.mult).then_inc(l1_step, 1)
                    dve.wait_ge(l1_step, at + 5)
                    dve.tensor_tensor(z[:, :], z[:, :], s2_bc[:, :], ALU.add).then_inc(l1_step, 1)
                    dve.wait_ge(l1_step, at + 6)
                    dve.tensor_reduce(small[:, 0:1], z[:, :], AX_X, ALU.max, negate=True).then_inc(z_ready, 1)
                    for q in range(4):
                        dve.wait_ge(p_tr, t * 4 + q + 1)
                        dve.tensor_copy(eT2[:, q * 512:(q + 1) * 512], bank[q % 2][:, :]).then_inc(pT_done, 1)
                    dve.wait_ge(p_done, t + 1)
                    dve.reciprocal(small[:, 2:3], small[:, 1:2]).then_inc(l1_step, 1)
                    dve.wait_ge(l1_step, at + 7)
                    dve.wait_ge(agg_done, t + 1)
                    dve.tensor_scalar(hid[:, :], bank[4][:, :], small[:, 2:3], None, ALU.mult).then_inc(agg_ready, 1)
                    dve.wait_ge(o_done, t + 1)
                    dve.tensor_tensor(e[:, :], bank[6][:, :], bv_bc[:, :], ALU.add).then_inc(l1_step, 1)
                    dve.wait_ge(l1_step, at + 8)
                    dve.wait_ge(x2_loaded, t * 16 + 16)
                    dve.scalar_tensor_tensor(y[:, :], e[:, :], 0.0, xt[:, :], ALU.max, ALU.add).then_inc(l1_step, 1)
                    dve.wait_ge(l1_step, at + 9)
                    dve.wait_ge(agg_ready, t + 1)
                    dve.memset(small[:, 7:8], 0.0).then_inc(o_ready, 1)
                    dve.wait_ge(out_stored, t * 16 + 16)

            @block.scalar
            def _(act):
                with act.Fori(0, T) as t:
                    act.wait_ge(u_done, t + 1)
                    for m in range(C):
                        act.activation(uT[:, m, :], bank[5][:, m * P:(m + 1) * P], ACT.Identity, bias=u_bias[:, m:m + 1])
                    act.activation(cT[:, :], bank[7][0:1, 0:P], ACT.Identity, bias=bqk[0:1, :]).then_inc(u_copied, 1)
                    act.wait_ge(z_ready, t + 1)
                    act.activation(z[:, :], z[:, :], ACT.Exp, bias=small[:, 0:1], accum_out=small[:, 1:2]).then_inc(p_done, 1)
                    act.wait_ge(aT_tr, t + 1)
                    act.activation(hT[:, 0, :], bank[5][:, :], ACT.Copy).then_inc(aT_done, 1)

            @block.tensor
            def _(pe):
                with pe.Fori(0, T) as t:
                    for m in range(C):
                        for c in range(C):
                            pe.matmul(bank[5][:, m * P:(m + 1) * P], w_qk[:, c, m * P:(m + 1) * P],
                                      h1T[:, c, :][:, bass.ds(t * P, P)], start=(c == 0), stop=(c == C - 1))
                    for c in range(C):
                        last = pe.matmul(bank[7][0:1, 0:P], c_vec[:, c:c + 1], h1T[:, c, :][:, bass.ds(t * P, P)],
                                         start=(c == 0), stop=(c == C - 1))
                    last.then_inc(u_done, 1)
                    pe.wait_ge(u_copied, t + 1)
                    for q in range(4):
                        for c in range(C):
                            pe.matmul(bank[q][:, :], uT[:, c, :], h1T[:, c, q * 512:(q + 1) * 512], start=(c == 0), stop=False)
                        pe.matmul(bank[q][:, :], cT[:, :], ones[0:1, :], start=False, stop=True).then_inc(z_done, 1)
                    pe.wait_ge(p_done, t + 1)
                    for q in range(4):
                        if q >= 2:
                            pe.wait_ge(pT_done, t * 4 + q - 1)
                        for i in range(4):
                            j = q * 4 + i
                            last = pe.transpose(bank[q % 2][:, i * P:(i + 1) * P], z[:, j * P:(j + 1) * P], ident[:, :])
                        last.then_inc(p_tr, 1)
                    pe.wait_ge(pT_done, t * 4 + 4)
                    for j in range(T):
                        last = pe.matmul(bank[4][:, :], eT2[:, j * P:(j + 1) * P], h1[:, j, :], start=(j == 0), stop=(j == T - 1))
                    last.then_inc(agg_done, 1)
                    pe.wait_ge(agg_ready, t + 1)
                    for c in range(C):
                        last = pe.transpose(bank[5][:, c * P:(c + 1) * P], hid[:, c * P:(c + 1) * P], ident[:, :])
                    last.then_inc(aT_tr, 1)
                    pe.wait_ge(aT_done, t + 1)
                    for c in range(C):
                        last = pe.matmul(bank[6][:, :], hT[:, 0, c * P:(c + 1) * P], wv_t[:, c, :],
                                         start=(c == 0), stop=(c == C - 1))
                    last.then_inc(o_done, 1)
                    pe.wait_ge(o_ready, t + 2)


_INS = ["x", "adj", "L0_gnn_W_seq", "L0_gnn_a1", "L0_gnn_a2", "L0_gnn_W_out", "L0_gnn_b_out", "L1_gnn_W_q",
        "L1_gnn_b_q", "L1_gnn_W_k", "L1_gnn_b_k", "L1_gnn_W_v", "L1_gnn_b_v"]


def kernel(**inputs):
    import numpy as _np
    import concourse.bacc as _bacc
    from concourse import mybir as _mybir
    from concourse.bass_utils import run_bass_kernel_spmd as _run

    nc = _bacc.Bacc("TRN2", target_bir_lowering=False, num_devices=1)
    arrays, args = {}, []
    for name in _INS:
        a = _np.ascontiguousarray(inputs[name])
        arrays[f"in_{name}_dram"] = a
        args.append(nc.dram_tensor(f"in_{name}_dram", a.shape, _mybir.dt.from_np(a.dtype), kind="ExternalInput").ap())
    out = nc.dram_tensor("out_0_dram", (N, D), F32, kind="ExternalOutput").ap()
    build(nc, *args, out)
    r = _run(nc, [arrays], core_ids=[0])
    return r.results[0]["out_0_dram"]
```
